# Optimizing a Trainium2 kernel written in Bass

```python
import numpy as np
import jax
import jax.numpy as jnp

def _softmax(x, axis=-1):
    return jax.nn.softmax(x, axis=axis)

def _gelu(x):
    return jax.nn.gelu(x, approximate=True)

def _silu(x):
    return jax.nn.silu(x)

def _sigmoid(x):
    return jax.nn.sigmoid(x)

def _layernorm(x, axis=-1, eps=1e-05):
    m = jnp.mean(x, axis=axis, keepdims=True)
    v = jnp.var(x, axis=axis, keepdims=True)
    return (x - m) / jnp.sqrt(v + eps)

def _scatter_add(tgt, idx, src, axis=0):
    return tgt.at[idx].add(src)

def _segment_sum(src, seg, n):
    return jax.ops.segment_sum(src, seg, n)
kernel_name = 'mk_macaron_d2_jaxref_r8_605f00'

def setup_inputs(seed: int=0):
    np.random.seed(seed)
    _w = jnp.asarray

    def _L0_attn_setup():
        import jax, jax.numpy as jnp
        import numpy as np
        import math
        HIDDEN = 128
        HEADS = 8
        HEAD = HIDDEN // HEADS
        B, S = (2, 256)
        SCALE_BASE = 64
        EPS = 1e-05

        def _xpos(x, downscale=False):
            d = x.shape[-1]
            s = x.shape[-2]
            half = d // 2
            scale_vec = (jnp.arange(0, d, 2, dtype=jnp.float32) + 0.4 * d) / (1.4 * d)
            pos = jnp.arange(s, dtype=jnp.float32)
            scale = scale_vec[None, :] ** (pos[:, None] / SCALE_BASE)
            inv_freq = 1.0 / 10000.0 ** (jnp.arange(half, dtype=jnp.float32) / half)
            ang = pos[:, None] * inv_freq[None, :]
            sin, cos = (jnp.sin(ang), jnp.cos(ang))
            if downscale:
                scale = 1.0 / scale
            sinp = jnp.repeat(sin * scale, 2, axis=-1)
            cosp = jnp.repeat(cos * scale, 2, axis=-1)
            x1, x2 = (x[..., ::2], x[..., 1::2])
            rot = jnp.stack([-x2, x1], axis=-1).reshape(x.shape)
            return x * cosp + rot * sinp

        def _gammas(h):
            return 1.0 - jnp.exp(jnp.linspace(math.log(1.0 / 32), math.log(1.0 / 64), h)).astype(jnp.float32)
        key = jax.random.key(seed)
        ks = jax.random.split(key, 6)
        X = jax.random.normal(ks[0], (B, S, HIDDEN), dtype=jnp.float32)
        W_Q = jax.random.normal(ks[1], (HEADS, HIDDEN, HEAD), dtype=jnp.float32) / HIDDEN
        W_K = jax.random.normal(ks[2], (HEADS, HIDDEN, HEAD), dtype=jnp.float32) / HIDDEN
        W_V = jax.random.normal(ks[3], (HEADS, HIDDEN, HEAD), dtype=jnp.float32) / HIDDEN
        W_G = jax.random.normal(ks[4], (HIDDEN, HIDDEN), dtype=jnp.float32) / HIDDEN
        W_O = jax.random.normal(ks[5], (HIDDEN, HIDDEN), dtype=jnp.float32) / HIDDEN
        gn_weight = jnp.ones((HIDDEN,), dtype=jnp.float32)
        gn_bias = jnp.zeros((HIDDEN,), dtype=jnp.float32)
        return dict(X=X, W_Q=W_Q, W_K=W_K, W_V=W_V, W_G=W_G, W_O=W_O, gn_weight=gn_weight, gn_bias=gn_bias)
    _L0_attn_in = _L0_attn_setup()

    def _L0_ffn_setup():
        import jax, jax.numpy as jnp
        import numpy as np
        INT4_QMAX = 7.0

        def simulate_quantize_int4(w):
            scale = jnp.max(jnp.abs(w)) / INT4_QMAX
            q = jnp.clip(jnp.round(w / scale), -8.0, 7.0)
            return q * scale
        key = jax.random.key(seed)
        k_x, k_w, k_bias, k_a, k_b = jax.random.split(key, 5)
        d_in, features, rank = (128, 128, 16)
        x = jax.random.normal(k_x, (4, 1024, d_in), dtype=jnp.float32)
        kernel = jax.random.normal(k_w, (d_in, features), dtype=jnp.float32)
        bias = jax.random.normal(k_bias, (features,), dtype=jnp.float32)
        a = jax.random.normal(k_a, (d_in, rank), dtype=jnp.float32) * (1.0 / np.sqrt(d_in))
        b = jax.random.normal(k_b, (rank, features), dtype=jnp.float32) * 0.01
        return {'x': x, 'kernel': kernel, 'bias': bias, 'a': a, 'b': b}
    _L0_ffn_in = _L0_ffn_setup()

    def _L1_attn_setup():
        import jax, jax.numpy as jnp
        import numpy as np
        D_MODEL = 128
        NUM_HEADS = 4
        EXPAND_K = 1.0
        EXPAND_V = 2.0
        KEY_DIM = int(D_MODEL * EXPAND_K)
        VALUE_DIM = int(D_MODEL * EXPAND_V)
        HEAD_K = KEY_DIM // NUM_HEADS
        HEAD_V = VALUE_DIM // NUM_HEADS
        CHUNK = 64
        EPS = 1e-05
        ROPE_BASE = 10000.0

        def _apply_rotary(q, k):
            d = q.shape[-1]
            half = d // 2
            inv_freq = 1.0 / ROPE_BASE ** (jnp.arange(0, d, 2, dtype=jnp.float32) / d)
            t = jnp.arange(q.shape[1], dtype=jnp.float32)
            freqs = t[:, None] * inv_freq[None, :]
            cos = jnp.cos(freqs)[None, :, None, :]
            sin = jnp.sin(freqs)[None, :, None, :]

            def rot(x):
                x1, x2 = (x[..., :half], x[..., half:])
                return jnp.concatenate([x1 * cos - x2 * sin, x2 * cos + x1 * sin], axis=-1)
            return (rot(q), rot(k))

        def _chunk_retention(q, k, v, gamma):
            B, T, H, dk = q.shape
            dv = v.shape[-1]
            C = CHUNK
            N = T // C
            qc = q.reshape(B, N, C, H, dk).transpose(1, 0, 3, 2, 4)
            kc = k.reshape(B, N, C, H, dk).transpose(1, 0, 3, 2, 4)
            vc = v.reshape(B, N, C, H, dv).transpose(1, 0, 3, 2, 4)
            i = jnp.arange(C, dtype=jnp.float32)
            cross_dec = gamma[:, None] ** (i + 1.0)
            k_dec = gamma[:, None] ** (C - 1.0 - i)
            diff = i[:, None] - i[None, :]
            mask = jnp.where(diff >= 0, gamma[:, None, None] ** diff, 0.0)
            gC = gamma ** C

            def step(S, inp):
                qb, kb, vb = inp
                attn = jnp.einsum('bhid,bhjd->bhij', qb, kb) * mask
                o_intra = jnp.einsum('bhij,bhjv->bhiv', attn, vb)
                o_inter = jnp.einsum('bhid,bhdv->bhiv', qb * cross_dec[:, :, None], S)
                S_new = gC[:, None, None] * S + jnp.einsum('bhjd,bhjv->bhdv', kb * k_dec[:, :, None], vb)
                return (S_new, o_intra + o_inter)
            S0 = jnp.zeros((B, H, dk, dv), dtype=q.dtype)
            _, o = jax.lax.scan(step, S0, (qc, kc, vc))
            return o.transpose(1, 0, 3, 2, 4).reshape(B, T, H, dv)
        key = jax.random.key(seed)
        ks = jax.random.split(key, 7)
        B, T = (4, 256)
        s = 0.02
        return {'x': jax.random.normal(ks[0], (B, T, D_MODEL), dtype=jnp.float32), 'Wq': jax.random.normal(ks[1], (KEY_DIM, D_MODEL), dtype=jnp.float32) * s, 'Wk': jax.random.normal(ks[2], (KEY_DIM, D_MODEL), dtype=jnp.float32) * s, 'Wv': jax.random.normal(ks[3], (VALUE_DIM, D_MODEL), dtype=jnp.float32) * s, 'Wg': jax.random.normal(ks[4], (VALUE_DIM, D_MODEL), dtype=jnp.float32) * s, 'Wo': jax.random.normal(ks[5], (D_MODEL, VALUE_DIM), dtype=jnp.float32) * s, 'gnorm_w': jnp.ones((HEAD_V,), dtype=jnp.float32)}
    _L1_attn_in = _L1_attn_setup()

    def _L1_ffn_setup():
        import jax, jax.numpy as jnp
        import numpy as np
        CAPACITY_FACTOR = 0.5
        key = jax.random.key(seed)
        ks = jax.random.split(key, 5)
        B, S, D, F = (4, 512, 128, 512)
        scale_in = 1.0 / np.sqrt(D)
        scale_ff = 1.0 / np.sqrt(F)
        return {'hidden_states': jax.random.normal(ks[0], (B, S, D), dtype=jnp.float32), 'w_router': jax.random.normal(ks[1], (D,), dtype=jnp.float32) * scale_in, 'W1': jax.random.normal(ks[2], (D, F), dtype=jnp.float32) * scale_in, 'b1': jnp.zeros((F,), dtype=jnp.float32), 'W2': jax.random.normal(ks[3], (F, D), dtype=jnp.float32) * scale_ff, 'b2': jnp.zeros((D,), dtype=jnp.float32)}
    _L1_ffn_in = _L1_ffn_setup()
    _d = {'L0_attn_X': _L0_attn_in['X'], 'L0_attn_W_Q': _L0_attn_in['W_Q'], 'L0_attn_W_K': _L0_attn_in['W_K'], 'L0_attn_W_V': _L0_attn_in['W_V'], 'L0_attn_W_G': _L0_attn_in['W_G'], 'L0_attn_W_O': _L0_attn_in['W_O'], 'L0_attn_gn_weight': _L0_attn_in['gn_weight'], 'L0_attn_gn_bias': _L0_attn_in['gn_bias'], 'L0_ffn_kernel': _L0_ffn_in['kernel'], 'L0_ffn_bias': _L0_ffn_in['bias'], 'L0_ffn_a': _L0_ffn_in['a'], 'L0_ffn_b': _L0_ffn_in['b'], 'L1_attn_Wq': _L1_attn_in['Wq'], 'L1_attn_Wk': _L1_attn_in['Wk'], 'L1_attn_Wv': _L1_attn_in['Wv'], 'L1_attn_Wg': _L1_attn_in['Wg'], 'L1_attn_Wo': _L1_attn_in['Wo'], 'L1_attn_gnorm_w': _L1_attn_in['gnorm_w'], 'L1_ffn_w_router': _L1_ffn_in['w_router'], 'L1_ffn_W1': _L1_ffn_in['W1'], 'L1_ffn_b1': _L1_ffn_in['b1'], 'L1_ffn_W2': _L1_ffn_in['W2'], 'L1_ffn_b2': _L1_ffn_in['b2']}
    _x0 = _d['L0_attn_X']
    _d['L0_attn_X'] = jax.random.normal(jax.random.fold_in(jax.random.key(seed), 1), (16, 512, 128), dtype=_x0.dtype)
    del _x0
    return _d

def reference(L0_attn_X, L0_attn_W_Q, L0_attn_W_K, L0_attn_W_V, L0_attn_W_G, L0_attn_W_O, L0_attn_gn_weight, L0_attn_gn_bias, L0_ffn_kernel, L0_ffn_bias, L0_ffn_a, L0_ffn_b, L1_attn_Wq, L1_attn_Wk, L1_attn_Wv, L1_attn_Wg, L1_attn_Wo, L1_attn_gnorm_w, L1_ffn_w_router, L1_ffn_W1, L1_ffn_b1, L1_ffn_W2, L1_ffn_b2):

    def _L0_attn_ref(X, W_Q, W_K, W_V, W_G, W_O, gn_weight, gn_bias):
        import jax, jax.numpy as jnp
        import numpy as np
        import math
        HIDDEN = 128
        HEADS = 8
        HEAD = HIDDEN // HEADS
        B, S = (2, 256)
        SCALE_BASE = 64
        EPS = 1e-05

        def _xpos(x, downscale=False):
            d = x.shape[-1]
            s = x.shape[-2]
            half = d // 2
            scale_vec = (jnp.arange(0, d, 2, dtype=jnp.float32) + 0.4 * d) / (1.4 * d)
            pos = jnp.arange(s, dtype=jnp.float32)
            scale = scale_vec[None, :] ** (pos[:, None] / SCALE_BASE)
            inv_freq = 1.0 / 10000.0 ** (jnp.arange(half, dtype=jnp.float32) / half)
            ang = pos[:, None] * inv_freq[None, :]
            sin, cos = (jnp.sin(ang), jnp.cos(ang))
            if downscale:
                scale = 1.0 / scale
            sinp = jnp.repeat(sin * scale, 2, axis=-1)
            cosp = jnp.repeat(cos * scale, 2, axis=-1)
            x1, x2 = (x[..., ::2], x[..., 1::2])
            rot = jnp.stack([-x2, x1], axis=-1).reshape(x.shape)
            return x * cosp + rot * sinp

        def _gammas(h):
            return 1.0 - jnp.exp(jnp.linspace(math.log(1.0 / 32), math.log(1.0 / 64), h)).astype(jnp.float32)
        b, s, _ = X.shape
        h, _, dv = W_V.shape
        Q = _xpos(jnp.einsum('bse,hed->bhsd', X, W_Q))
        K = _xpos(jnp.einsum('bse,hed->bhsd', X, W_K), downscale=True)
        V = jnp.einsum('bse,hed->bhsd', X, W_V)
        gam = _gammas(h)
        n = jnp.arange(s)
        diff = n[:, None] - n[None, :]
        mask = diff >= 0
        D = jnp.where(mask[None], gam[:, None, None] ** jnp.where(mask, diff, 0)[None].astype(jnp.float32), 0.0)
        scores = jnp.einsum('bhsd,bhtd->bhst', Q, K) * D[None]
        Y = jnp.einsum('bhst,bhtv->bhsv', scores, V)
        Y = jnp.transpose(Y, (0, 2, 1, 3))
        mu = Y.mean(-1, keepdims=True)
        var = Y.var(-1, keepdims=True)
        Yn = ((Y - mu) / jnp.sqrt(var + EPS)).reshape(b, s, h * dv) * gn_weight + gn_bias
        gate = X @ W_G
        gate = gate * jax.nn.sigmoid(gate)
        return gate * Yn @ W_O

    def _L0_ffn_ref(x, kernel, bias, a, b):
        import jax, jax.numpy as jnp
        import numpy as np
        INT4_QMAX = 7.0

        def simulate_quantize_int4(w):
            scale = jnp.max(jnp.abs(w)) / INT4_QMAX
            q = jnp.clip(jnp.round(w / scale), -8.0, 7.0)
            return q * scale
        w = simulate_quantize_int4(kernel)
        y = jnp.einsum('bsd,df->bsf', x, w) + bias
        lora = jnp.einsum('bsr,rf->bsf', jnp.einsum('bsd,dr->bsr', x, a), b)
        return y + lora

    def _L1_attn_ref(x, Wq, Wk, Wv, Wg, Wo, gnorm_w):
        import jax, jax.numpy as jnp
        import numpy as np
        D_MODEL = 128
        NUM_HEADS = 4
        EXPAND_K = 1.0
        EXPAND_V = 2.0
        KEY_DIM = int(D_MODEL * EXPAND_K)
        VALUE_DIM = int(D_MODEL * EXPAND_V)
        HEAD_K = KEY_DIM // NUM_HEADS
        HEAD_V = VALUE_DIM // NUM_HEADS
        CHUNK = 64
        EPS = 1e-05
        ROPE_BASE = 10000.0

        def _apply_rotary(q, k):
            d = q.shape[-1]
            half = d // 2
            inv_freq = 1.0 / ROPE_BASE ** (jnp.arange(0, d, 2, dtype=jnp.float32) / d)
            t = jnp.arange(q.shape[1], dtype=jnp.float32)
            freqs = t[:, None] * inv_freq[None, :]
            cos = jnp.cos(freqs)[None, :, None, :]
            sin = jnp.sin(freqs)[None, :, None, :]

            def rot(x):
                x1, x2 = (x[..., :half], x[..., half:])
                return jnp.concatenate([x1 * cos - x2 * sin, x2 * cos + x1 * sin], axis=-1)
            return (rot(q), rot(k))

        def _chunk_retention(q, k, v, gamma):
            B, T, H, dk = q.shape
            dv = v.shape[-1]
            C = CHUNK
            N = T // C
            qc = q.reshape(B, N, C, H, dk).transpose(1, 0, 3, 2, 4)
            kc = k.reshape(B, N, C, H, dk).transpose(1, 0, 3, 2, 4)
            vc = v.reshape(B, N, C, H, dv).transpose(1, 0, 3, 2, 4)
            i = jnp.arange(C, dtype=jnp.float32)
            cross_dec = gamma[:, None] ** (i + 1.0)
            k_dec = gamma[:, None] ** (C - 1.0 - i)
            diff = i[:, None] - i[None, :]
            mask = jnp.where(diff >= 0, gamma[:, None, None] ** diff, 0.0)
            gC = gamma ** C

            def step(S, inp):
                qb, kb, vb = inp
                attn = jnp.einsum('bhid,bhjd->bhij', qb, kb) * mask
                o_intra = jnp.einsum('bhij,bhjv->bhiv', attn, vb)
                o_inter = jnp.einsum('bhid,bhdv->bhiv', qb * cross_dec[:, :, None], S)
                S_new = gC[:, None, None] * S + jnp.einsum('bhjd,bhjv->bhdv', kb * k_dec[:, :, None], vb)
                return (S_new, o_intra + o_inter)
            S0 = jnp.zeros((B, H, dk, dv), dtype=q.dtype)
            _, o = jax.lax.scan(step, S0, (qc, kc, vc))
            return o.transpose(1, 0, 3, 2, 4).reshape(B, T, H, dv)
        B, T, _ = x.shape
        H = NUM_HEADS
        q = (x @ Wq.T).reshape(B, T, H, HEAD_K)
        k = (x @ Wk.T).reshape(B, T, H, HEAD_K)
        v = (x @ Wv.T).reshape(B, T, H, HEAD_V)
        g = (x @ Wg.T).reshape(B, T, H, HEAD_V)
        q, k = _apply_rotary(q, k)
        q = q * HEAD_K ** (-0.5)
        gamma = 1.0 - jnp.exp2(-5.0 - jnp.arange(H, dtype=jnp.float32))
        o = _chunk_retention(q, k, v, gamma)
        var = jnp.mean(o * o, axis=-1, keepdims=True)
        o = o * jax.lax.rsqrt(var + EPS) * gnorm_w
        o = o * (g * jax.nn.sigmoid(g))
        return o.reshape(B, T, H * HEAD_V) @ Wo.T

    def _L1_ffn_ref(hidden_states, w_router, W1, b1, W2, b2):
        import jax, jax.numpy as jnp
        import numpy as np
        CAPACITY_FACTOR = 0.5
        'Mixture-of-Depths block: route top-k tokens through an FFN inner block,\n            scatter back with sigmoid router weights; bypassed tokens pass through.'
        B, S, D = hidden_states.shape
        k = int(S * CAPACITY_FACTOR)
        scores = jnp.einsum('bsd,d->bs', hidden_states, w_router)
        top_scores, top_idx = jax.lax.top_k(scores, k)
        weights = jax.nn.sigmoid(top_scores)
        selected = jnp.take_along_axis(hidden_states, top_idx[:, :, None], axis=1)
        h = jax.nn.gelu(jnp.einsum('bkd,df->bkf', selected, W1) + b1)
        processed = jnp.einsum('bkf,fd->bkd', h, W2) + b2
        update = weights[:, :, None] * processed

        def scatter_one(xb, ib, ub):
            return xb.at[ib].add(ub)
        output = jax.vmap(scatter_one)(hidden_states, top_idx, update)
        return output
    x = L0_attn_X
    x = x + 0.5 * _L0_ffn_ref(_layernorm(x, axis=-1), L0_ffn_kernel, L0_ffn_bias, L0_ffn_a, L0_ffn_b)
    x = x + _L0_attn_ref(_layernorm(x, axis=-1), L0_attn_W_Q, L0_attn_W_K, L0_attn_W_V, L0_attn_W_G, L0_attn_W_O, L0_attn_gn_weight, L0_attn_gn_bias)
    x = x + 0.5 * _L0_ffn_ref(_layernorm(x, axis=-1), L0_ffn_kernel, L0_ffn_bias, L0_ffn_a, L0_ffn_b)
    x = x + 0.5 * _L1_ffn_ref(_layernorm(x, axis=-1), L1_ffn_w_router, L1_ffn_W1, L1_ffn_b1, L1_ffn_W2, L1_ffn_b2)
    x = x + _L1_attn_ref(_layernorm(x, axis=-1), L1_attn_Wq, L1_attn_Wk, L1_attn_Wv, L1_attn_Wg, L1_attn_Wo, L1_attn_gnorm_w)
    x = x + 0.5 * _L1_ffn_ref(_layernorm(x, axis=-1), L1_ffn_w_router, L1_ffn_W1, L1_ffn_b1, L1_ffn_W2, L1_ffn_b2)
    return x

_drawn_inputs = setup_inputs


def setup_inputs(seed=0):
    import zlib

    import numpy as np

    out = dict(_drawn_inputs(seed))
    spreads = {'L0_attn_gn_weight': (1.0, 0.6),
     'L0_attn_gn_bias': (0.0, 0.8),
     'L1_attn_gnorm_w': (1.0, 0.6),
     'L1_ffn_b1': (0.0, 2.0),
     'L1_ffn_b2': (0.0, 0.8)}
    factors = {'L0_attn_W_Q': 8.0,
     'L0_attn_W_K': 8.0,
     'L0_attn_W_V': 8.0,
     'L0_attn_W_G': 8.0,
     'L0_attn_W_O': 8.0,
     'L0_ffn_a': 8.0,
     'L0_ffn_b': 8.0,
     'L1_attn_Wq': 8.0,
     'L1_attn_Wk': 8.0,
     'L1_attn_Wv': 8.0,
     'L1_attn_Wg': 8.0,
     'L1_attn_Wo': 8.0}
    for name, (base, spread) in spreads.items():
        noise = np.random.default_rng([zlib.crc32(name.encode()), seed]).standard_normal(out[name].shape)
        drawn = base * np.exp(spread * noise) if base else spread * noise
        out[name] = jnp.asarray(drawn.astype(out[name].dtype))
    for name, factor in factors.items():
        out[name] = (out[name] * factor).astype(out[name].dtype)
    return out
```

```python
from contextlib import ExitStack

import numpy as np

import concourse.bass as bass
from concourse import mybir

ALU = mybir.AluOpType
ACT = mybir.ActivationFunctionType
AX = mybir.AxisListType
F32 = mybir.dt.float32
BF16 = mybir.dt.bfloat16
I32 = mybir.dt.int32

P = 128
NB, NT = 16, 4
S = NT * P
G = 2
EPS = 1e-5
H0, E0 = 8, 16
H1, K1, V1 = 4, 32, 64
VF = H1 * V1
FH = 512
NF = FH // P
TOPK = S // 2
REP, ROUNDS = 8, 8
BANK = 512
BK = 96

LN_STEPS = ("stats", "mv", "sq", "ve", "rstd", "xn", "t", "xt")


def program(nc, x, wq0, wk0, wv0, wg0, wo0, gnw, gnb, kern, bias, fa, fb,
            wq1, wk1, wv1, wg1, wo1, gcol, wr, w1, b1, w2, b2,
            ident_d, tri_d, bd0_d, bd1_d, par_d, rot0_d, rot1_d, blk_d, rs_d, out):
    with ExitStack() as ctx:
        def sb(name, shape, dt=F32):
            return ctx.enter_context(nc.sbuf_tensor(name, shape, dt))

        def sem(name):
            return ctx.enter_context(nc.semaphore(name))

        ident = sb("ident", [P, P])
        tri = sb("tri", [P, P])
        bd0 = sb("bd0", [P, P])
        bd1 = sb("bd1", [P, VF])
        par = sb("par", [P, 2])
        rot0 = sb("rot0", [P, 2, 2 * S])
        rot1 = sb("rot1", [P, 2, 2 * S])
        blk = sb("blk", [P, P])
        rs = sb("rs", [P, ROUNDS])
        blkb = sb("blkb", [P, P], BF16)
        ones_b = sb("ones_b", [BK, P], BF16)
        w_qkvg = sb("w_qkvg", [P, 4, P])
        w_o0 = sb("w_o0", [P, P])
        gnw_b = sb("gnw_b", [P, P])
        gnb_b = sb("gnb_b", [P, P])
        kern_s = sb("kern_s", [P, P])
        fa_s = sb("fa_s", [P, 16])
        fb_s = sb("fb_s", [16, P])
        faT = sb("faT", [16, P])
        amax = sb("amax", [P, 4])
        vmean = sb("vmean", [P, H0])
        w_ffn = sb("w_ffn", [P, P])
        brow = sb("brow", [1, 2, P])
        bres = sb("bres", [1, 2, 2, P])
        bias_f = sb("bias_f", [BK, NT, P], BF16)
        bias_2 = sb("bias_2", [BK, NT, P], BF16)
        w_qkv1 = sb("w_qkv1", [P, 2 * P + VF])
        w_g1 = sb("w_g1", [P, VF])
        w_o1 = sb("w_o1", [P, 2, P])
        gcol_s = sb("gcol_s", [P, 1])
        wr_s = sb("wr_s", [P, 1])
        w1_s = sb("w1_s", [P, NF, P])
        b1_s = sb("b1_s", [P, NF])
        w2_s = sb("w2_s", [P, NF, P])
        mhalf = sb("mhalf", [P, 32])

        base = sb("base", [P, NB * S])
        yall = sb("yall", [P, NB * S])
        scol = sb("scol", [P, NB * NT])
        wcol = sb("wcol", [P, NB * NT])

        def per(name, shape):
            return [sb(f"{name}{u}", shape) for u in range(G)]

        xin = per("xin", [P, NT, P])
        xw = per("xw", [P, NT, P])
        xn = per("xn", [P, NT, P])
        xt = per("xt", [P, NT, P])
        st6 = per("st6", [P, NT, 6])
        mv = per("mv", [P, 5, NT])
        ve = per("ve", [P, 32])
        rstd = per("rstd", [P, 32])
        qkr = per("qkr", [P, 2, NT, P])
        vv = per("vv", [P, NT, VF])
        gate = per("gate", [P, NT * VF])
        qt = per("qt", [P, S])
        kt = per("kt", [P, 2, S])
        big = per("big", [P, 8 * S])
        um = per("um", [P, 3, VF])
        t2 = per("t2", [P, NT * VF])
        PS = [ctx.enter_context(nc.psum_tensor(f"ps{u}", [P, 4 * BANK], F32)) for u in range(G)]

        def bank(u, k, a=0, n=BANK):
            return PS[u][:, k * BANK + a:k * BANK + a + n]

        ra = [big[u][:, 0:2 * S] for u in range(G)]
        rb = [big[u][:, 2 * S:4 * S] for u in range(G)]
        th = [big[u][:, 4 * S:6 * S] for u in range(G)]
        sc = [big[u][:, :].rearrange("p (h n) -> p h n", h=8) for u in range(G)]
        hid = [big[u][:, 0:NF * S].rearrange("p (f n) -> p f n", f=NF) for u in range(G)]
        srow, rankb = big[0][:, 0:S], big[0][:, S:2 * S]
        msk_a, msk_b, pre, zero = (big[0][:, k * S:(k + 1) * S] for k in range(2, 6))
        srep = big[1][:, 0:S].rearrange("p (j b r) -> p j b r", j=NT, b=NB)

        names = []
        for st in ("ln1", "ln2", "ln3", "ln4", "ln5", "ln6"):
            names += [f"{st}_{k}" for k in LN_STEPS]
        for a in ("a", "b"):
            names += [f"{a}_{k}" for k in (
                "qkvg", "v", "tanh", "prod", "gate", "qkr", "tqk", "qkt", "state", "um", "um1",
                "state_sum", "y", "sq", "var", "gve", "grstd", "yn", "gy", "tg", "gt", "wo",
                "score", "score_c", "h", "act", "mod", "ystore", "base")]
        names += [f"x_in{u}" for u in range(G)]
        names += ["a_ffn1", "xin_free", "a_x1", "a_x2", "a_ffn3", "a_x3", "a_ynw", "a_ynb",
                  "a_sc_e", "a_msk_e", "a_sc_o", "a_msk_o", "b_x4", "b_x5", "b_g", "b_sc", "b_msk",
                  "c_out", "c_store",
                  "w_load", "w_step", "w_pool", "w_pe", "w_act",
                  "k_dve", "k_pe", "k_act"]
        s = {n: sem(n) for n in names}

        block = ctx.enter_context(nc.Block())

        def counts(eng, i):
            return [eng.snap(i * G + (u + 1)) for u in range(G)], eng.snap(i * G + FREE)

        @block.sync
        def _(sp):
            sp.sem_inc(s["c_store"], FREE)
            def load(dst, src):
                sp.dma_start(dst, src).then_inc(s["w_load"], 16)
            with nc.allow_non_contiguous_dma("weights, once"):
                load(ident[:], ident_d)
                load(kern_s[:], kern)
                load(fa_s[:], fa)
                load(fb_s[:], fb)
                load(brow[0:1, 0, :], bias.rearrange("(a n) -> a n", a=1))
                load(brow[0:1, 1, :], b2.rearrange("(a n) -> a n", a=1))
                for n, w in enumerate((wq0, wk0, wv0)):
                    load(w_qkvg[:, n, :].rearrange("p (h e) -> p h e", h=H0), w.rearrange("h p e -> p h e"))
                load(w_qkvg[:, 3, :], wg0)
                load(w_o0[:], wo0)
                load(gnw_b[:], gnw.rearrange("(a n) -> a n", a=1).to_broadcast((P, P)))
                load(gnb_b[:], gnb.rearrange("(a n) -> a n", a=1).to_broadcast((P, P)))
                load(w_qkv1[:, 0:P], wq1)
                load(w_qkv1[:, P:2 * P], wk1)
                load(w_qkv1[:, 2 * P:], wv1)
                load(w_g1[:], wg1)
                load(w_o1[:], wo1.rearrange("(k p) n -> p k n", p=P))
                load(gcol_s[:], gcol)
                load(wr_s[:], wr.rearrange("(p a) -> p a", a=1))
                load(w1_s[:].rearrange("p f n -> p (f n)"), w1)
                load(b1_s[:], b1.rearrange("(f p) -> p f", p=P))
                load(w2_s[:], w2.rearrange("(f p) n -> p f n", p=P))
                load(tri[:], tri_d)
                load(bd0[:], bd0_d)
                load(bd1[:], bd1_d)
                load(par[:], par_d)
                load(rot0[:].rearrange("p a n -> p (a n)"), rot0_d)
                load(rot1[:].rearrange("p a n -> p (a n)"), rot1_d)
                load(blk[:], blk_d)
                load(rs[:], rs_d)
            with sp.Fori(0, NB // G) as i:
                _, past = counts(sp, i)
                for u in range(G):
                    sp.wait_ge(s["xin_free"], past)
                    sp.dma_start(xin[u][:], x[bass.ds(i * G + u, 1)].rearrange("a (j p) n -> (a p) j n", p=P)) \
                        .then_inc(s[f"x_in{u}"], 16)
            with sp.Fori(0, NB // G) as i:
                now, _ = counts(sp, i)
                for u in range(G):
                    sp.wait_ge(s["c_out"], now[u])
                    sp.dma_start(out[bass.ds(i * G + u, 1)].rearrange("a (j p) n -> (a p) j n", p=P), xw[u][:]) \
                        .then_inc(s["c_store"], 16)
            sp.wait_ge(s["c_store"], 16 * NB + FREE)

        N_LOADS = 31

        @block.tensor
        def _(pe):
            def transpose4(u, st, src, k, now):
                pe.wait_ge(s[f"{st}_xn"], now)
                for j in range(NT):
                    mm = nc.tensor.transpose(bank(u, k, j * P, P), src[:, j, :], ident[:])
                mm.then_inc(s[f"{st}_t"], 1)

            def ffn(u, st, now, signal):
                nc.tensor.matmul(bank(u, 1), ones_b[:], bias_f[:].rearrange("p j n -> p (j n)"),
                                 start=True, stop=False, skip_group_check=True)
                pe.wait_ge(s[f"{st}_xt"], now)
                for j in range(NT):
                    mm = nc.tensor.matmul(bank(u, 1, j * P, P), xt[u][:, j, :], w_ffn[:],
                                          start=False, stop=(j == NT - 1), skip_group_check=True)
                mm.then_inc(s[signal], 1)

            def routed(u, a, st, now):
                transpose4(u, st, xn[u], 0, now)
                pe.wait_ge(s[f"{st}_xt"], now)
                for j in range(NT):
                    mm = nc.tensor.matmul(bank(u, 1, j, 1), xt[u][:, j, :], wr_s[:], start=True, stop=True,
                                          skip_group_check=True)
                mm.then_inc(s[f"{a}_score"], 1)

            def routed_up(u, a, now):
                for f in range(NF):
                    k = (f + 2) % 4
                    if k == 1:
                        pe.wait_ge(s[f"{a}_score_c"], now)
                    nc.tensor.matmul(bank(u, k), w1_s[:, f, :], xt[u][:].rearrange("p j n -> p (j n)"),
                                     start=True, stop=True).then_inc(s[f"{a}_h"], 1)

            def routed_down(u, a, now4):
                for f in range(NF):
                    pe.wait_ge(s[f"{a}_act"], now4 - (NF - 1 - f))
                    if f == 0:
                        nc.tensor.matmul(bank(u, 2), ones_b[:], bias_2[:].rearrange("p j n -> p (j n)"),
                                         start=True, stop=False, skip_group_check=True)
                    for j in range(NT):
                        mm = nc.tensor.matmul(bank(u, 2, j * P, P), hid[u][:, f, j * P:(j + 1) * P],
                                              w2_s[:, f, :], start=False, stop=(f == NF - 1 and j == NT - 1),
                                              skip_group_check=True)
                mm.then_inc(s[f"{a}_mod"], 1)

            pe.wait_ge(s["w_load"], 16 * N_LOADS)
            nc.tensor.transpose(PS[0][0:16, 0:P], fa_s[:], ident[:]).then_inc(s["w_pe"], 1)
            pe.wait_ge(s["w_act"], 1)
            nc.tensor.matmul(PS[0][:, BANK:BANK + P], faT[:], fb_s[:], start=True, stop=True) \
                .then_inc(s["w_pe"], 1)
            pe.wait_ge(s["w_step"], W_STEPS)
            pe.wait_ge(s["w_pool"], W_POOL)

            with pe.Fori(0, NB // G) as i:
                now, past = counts(pe, i)
                now4 = [pe.snap((i * G + u + 1) * NF) for u in range(G)]
                for u in range(G):
                    transpose4(u, "ln1", xn[u], 0, now[u])
                for u in range(G):
                    ffn(u, "ln1", now[u], "a_ffn1")
                for u in range(G):
                    transpose4(u, "ln2", xn[u], 0, now[u])
                for u in range(G):
                    pe.wait_ge(s["a_ystore"], past)
                    pe.wait_ge(s["ln2_xt"], now[u])
                    for k in range(4):
                        for j in range(NT):
                            mm = nc.tensor.matmul(bank(u, k, j * P, P), xt[u][:, j, :], w_qkvg[:, k, :],
                                                  start=True, stop=True, skip_group_check=True)
                    mm.then_inc(s["a_qkvg"], 1)
                for u in range(G):
                    pe.wait_ge(s["a_qkr"], now[u])
                    pe.wait_ge(s["a_v"], now[u])
                    pe.wait_ge(s["a_gate"], now[u])
                    for q in range(2):
                        for j in range(NT):
                            mm = nc.tensor.transpose(bank(u, q, j * P, P), qkr[u][:, q, j, :], ident[:])
                    mm.then_inc(s["a_tqk"], 1)
                    for c in range(NT - 1):
                        mm = nc.tensor.matmul(bank(u, 2, c * P, P), qkr[u][:, 1, c, :], vv[u][:, c, 0:P],
                                              start=True, stop=True, skip_group_check=True)
                    mm.then_inc(s["a_state"], 1)
                for parity in range(2):
                    for u in range(G):
                        if parity == 0:
                            pe.wait_ge(s["a_qkt"], now[u])
                            pe.wait_ge(s["a_um"], now[u])
                        else:
                            pe.wait_ge(s["a_msk_e"], now[u])
                        for c in range(NT):
                            for g in range(4):
                                r, t = slice(32 * g, 32 * g + 32), slice(c * P, (c + 1) * P)
                                mm = nc.tensor.matmul(bank(u, g, c * P, P), kt[u][r, parity, t], qt[u][r, t],
                                                      start=True, stop=True, skip_group_check=True)
                        mm.then_inc(s["a_sc_o" if parity else "a_sc_e"], 1)
                for u in range(G):
                    pe.wait_ge(s["a_msk_o"], now[u])
                    pe.wait_ge(s["a_state_sum"], now[u])
                    for c in range(NT):
                        t = slice(c * P, (c + 1) * P)
                        if c:
                            nc.tensor.matmul(bank(u, 0, c * P, P), qt[u][:, t], um[u][:, c - 1, 0:P],
                                             start=True, stop=False, skip_group_check=True)
                        for h in range(H0):
                            mm = nc.tensor.matmul(bank(u, 0, c * P + h * E0, E0), sc[u][:, h, t],
                                                  vv[u][:, c, h * E0:(h + 1) * E0],
                                                  start=(c == 0 and h == 0), stop=(h == H0 - 1),
                                                  skip_group_check=True)
                    mm.then_inc(s["a_y"], 1)
                for u in range(G):
                    pe.wait_ge(s["a_gy"], now[u])
                    for j in range(NT):
                        mm = nc.tensor.transpose(bank(u, 1, j * P, P), t2[u][:, j * P:(j + 1) * P], ident[:])
                    mm.then_inc(s["a_tg"], 1)
                for u in range(G):
                    pe.wait_ge(s["a_gt"], now[u])
                    for j in range(NT):
                        mm = nc.tensor.matmul(bank(u, 2, j * P, P), qt[u][:, j * P:(j + 1) * P], w_o0[:],
                                              start=True, stop=True, skip_group_check=True)
                    mm.then_inc(s["a_wo"], 1)
                for u in range(G):
                    transpose4(u, "ln3", xn[u], 3, now[u])
                for u in range(G):
                    ffn(u, "ln3", now[u], "a_ffn3")
                for u in range(G):
                    routed(u, "a", "ln4", now[u])
                for u in range(G):
                    routed_up(u, "a", now[u])
                for u in range(G):
                    routed_down(u, "a", now4[u])

            def topk(n0):
                pe.wait_ge(s["k_dve"], n0 + 1)
                for j in range(NT):
                    mm = nc.tensor.transpose(PS[0][:, j * P:(j + 1) * P], big[1][:, j * P:(j + 1) * P], ident[:])
                mm.then_inc(s["k_pe"], 1)
                for r in range(ROUNDS):
                    pe.wait_ge(s["k_dve"], n0 + K_HEAD + K_ROUND * r + K_ROUND - 1)
                    nc.tensor.matmul(PS[0][:, BANK:BANK + 1], blkb[:], rankb.bitcast(BF16)[:, 0:1],
                                     start=True, stop=True).then_inc(s["k_pe"], 1)
                pe.wait_ge(s["k_dve"], n0 + K_STEPS - 1)
                for j in range(NT):
                    mm = nc.tensor.transpose(PS[0][:, j * P:(j + 1) * P], msk_a[:, j * P:(j + 1) * P], ident[:])
                mm.then_inc(s["k_pe"], 1)

            pe.wait_ge(s["a_ystore"], NB + FREE)
            topk(0)
            pe.wait_ge(s["k_dve"], K_STEPS)

            with pe.Fori(0, NB // G) as i:
                now, past = counts(pe, i)
                now4 = [pe.snap((i * G + u + 1) * NF) for u in range(G)]
                for u in range(G):
                    transpose4(u, "ln5", xn[u], 0, now[u])
                for u in range(G):
                    pe.wait_ge(s["b_ystore"], past)
                    pe.wait_ge(s["ln5_xt"], now[u])
                    for k in range(2):
                        for j in range(NT):
                            nc.tensor.matmul(bank(u, k, j * P, P), xt[u][:, j, :], w_qkv1[:, k * P:(k + 1) * P],
                                             start=True, stop=True, skip_group_check=True)
                    for j in range(NT):
                        mm = nc.tensor.matmul(bank(u, 2 + j // 2, (j % 2) * VF, VF), xt[u][:, j, :],
                                              w_qkv1[:, 2 * P:], start=True, stop=True, skip_group_check=True)
                    mm.then_inc(s["b_qkvg"], 1)
                for u in range(G):
                    pe.wait_ge(s["b_prod"], now[u])
                    pe.wait_ge(s["b_v"], now[u])
                    for j in range(NT):
                        mm = nc.tensor.matmul(bank(u, j // 2, (j % 2) * VF, VF), xt[u][:, j, :], w_g1[:],
                                              start=True, stop=True, skip_group_check=True)
                    mm.then_inc(s["b_g"], 1)
                for u in range(G):
                    pe.wait_ge(s["b_qkr"], now[u])
                    for q in range(2):
                        for j in range(NT):
                            mm = nc.tensor.transpose(bank(u, 2 + q, j * P, P), qkr[u][:, q, j, :], ident[:])
                    mm.then_inc(s["b_tqk"], 1)
                for u in range(G):
                    pe.wait_ge(s["b_gate"], now[u])
                    for c in range(NT - 1):
                        mm = nc.tensor.matmul(bank(u, c // 2, (c % 2) * VF, VF), qkr[u][:, 1, c, :], vv[u][:, c, :],
                                              start=True, stop=True, skip_group_check=True)
                    mm.then_inc(s["b_state"], 1)
                for u in range(G):
                    pe.wait_ge(s["b_qkt"], now[u])
                    pe.wait_ge(s["b_um"], now[u])
                    for c in range(NT):
                        for g in range(H1):
                            r, t = slice(32 * g, 32 * g + 32), slice(c * P, (c + 1) * P)
                            mm = nc.tensor.matmul(bank(u, g, c * P, P), kt[u][r, 0, t], qt[u][r, t],
                                                  start=True, stop=True, skip_group_check=True)
                    mm.then_inc(s["b_sc"], 1)
                for u in range(G):
                    pe.wait_ge(s["b_msk"], now[u])
                    pe.wait_ge(s["b_state_sum"], now[u])
                    for c in range(NT):
                        t = slice(c * P, (c + 1) * P)
                        if c:
                            nc.tensor.matmul(bank(u, c // 2, (c % 2) * VF, VF), qt[u][:, t], um[u][:, c - 1, :],
                                             start=True, stop=False, skip_group_check=True)
                        for h in range(H1):
                            mm = nc.tensor.matmul(bank(u, c // 2, (c % 2) * VF + h * V1, V1), sc[u][:, h, t],
                                                  vv[u][:, c, h * V1:(h + 1) * V1],
                                                  start=(c == 0 and h == 0), stop=(h == H1 - 1),
                                                  skip_group_check=True)
                    mm.then_inc(s["b_y"], 1)
                for u in range(G):
                    pe.wait_ge(s["b_gy"], now[u])
                    for k in range(2):
                        for j in range(NT):
                            mm = nc.tensor.transpose(bank(u, 2 + k, j * P, P),
                                                     t2[u][:, j * VF + k * P:j * VF + (k + 1) * P], ident[:])
                    mm.then_inc(s["b_tg"], 1)
                for u in range(G):
                    pe.wait_ge(s["b_gt"], now[u])
                    for j in range(NT):
                        for k in range(2):
                            mm = nc.tensor.matmul(bank(u, 0, j * P, P), kt[u][:, k, j * P:(j + 1) * P], w_o1[:, k, :],
                                                  start=(k == 0), stop=(k == 1), skip_group_check=True)
                    mm.then_inc(s["b_wo"], 1)
                for u in range(G):
                    routed(u, "b", "ln6", now[u])
                for u in range(G):
                    routed_up(u, "b", now[u])
                for u in range(G):
                    routed_down(u, "b", now4[u])

            pe.wait_ge(s["b_ystore"], NB + FREE)
            topk(K_STEPS)

        @block.scalar
        def _(act):
            act.sem_inc(s["a_ystore"], FREE)
            act.sem_inc(s["b_ystore"], FREE)

            def copy_xt(u, st, k, now):
                act.wait_ge(s[f"{st}_t"], now)
                nc.scalar.copy(xt[u][:].rearrange("p j n -> p (j n)"), bank(u, k)).then_inc(s[f"{st}_xt"], 1)

            def hidden(u, a, now4):
                for f in range(NF):
                    act.wait_ge(s[f"{a}_h"], now4 - (NF - 1 - f))
                    nc.scalar.activation(hid[u][:, f, :], bank(u, (f + 2) % 4), ACT.Gelu_apprx_tanh,
                                         bias=b1_s[:, f:f + 1]).then_inc(s[f"{a}_act"], 1)

            def store_y(u, a, i, now):
                act.wait_ge(s[f"{a}_mod"], now)
                nc.scalar.copy(yall[:, bass.ds((i * G + u) * S, S)], bank(u, 2)).then_inc(s[f"{a}_ystore"], 1)

            act.wait_ge(s["w_pe"], 1)
            nc.scalar.copy(faT[:], PS[0][0:16, 0:P]).then_inc(s["w_act"], 1)
            act.wait_ge(s["w_load"], 16 * N_LOADS)

            with act.Fori(0, NB // G) as i:
                now, past = counts(act, i)
                now4 = [act.snap((i * G + u + 1) * NF) for u in range(G)]
                for u in range(G):
                    copy_xt(u, "ln1", 0, now[u])
                for u in range(G):
                    copy_xt(u, "ln2", 0, now[u])
                for u in range(G):
                    act.wait_ge(s["a_qkvg"], now[u])
                    nc.scalar.activation(th[u][:, 0:S], bank(u, 3), ACT.Tanh, scale=0.5).then_inc(s["a_tanh"], 1)
                    nc.scalar.copy(vv[u][:, :, 0:P], bank(u, 2).rearrange("p (j n) -> p j n", j=NT)).then_inc(s["a_v"], 1)
                for u in range(G):
                    act.wait_ge(s["a_tqk"], now[u])
                    nc.scalar.copy(qt[u][:], bank(u, 0))
                    nc.scalar.activation(kt[u][:, 0, :], bank(u, 1), ACT.Copy, scale=par[:, 0:1])
                    nc.scalar.activation(kt[u][:, 1, :], bank(u, 1), ACT.Copy, scale=par[:, 1:2]) \
                        .then_inc(s["a_qkt"], 1)
                for u in range(G):
                    act.wait_ge(s["a_y"], now[u])
                    nc.scalar.activation(t2[u][:, S:2 * S], bank(u, 0), ACT.Square).then_inc(s["a_sq"], 1)
                for u in range(G):
                    act.wait_ge(s["a_tg"], now[u])
                    nc.scalar.copy(qt[u][:], bank(u, 1)).then_inc(s["a_gt"], 1)
                for u in range(G):
                    copy_xt(u, "ln3", 3, now[u])
                for u in range(G):
                    copy_xt(u, "ln4", 0, now[u])
                for u in range(G):
                    hidden(u, "a", now4[u])
                for u in range(G):
                    store_y(u, "a", i, now[u])

            act.wait_ge(s["a_score_c"], NB)
            nc.scalar.activation(wcol[:], scol[:], ACT.Tanh, scale=0.5).then_inc(s["k_act"], 1)

            with act.Fori(0, NB // G) as i:
                now, past = counts(act, i)
                now4 = [act.snap((i * G + u + 1) * NF) for u in range(G)]
                for u in range(G):
                    copy_xt(u, "ln5", 0, now[u])
                for u in range(G):
                    act.wait_ge(s["b_qkvg"], now[u])
                    nc.scalar.copy(vv[u][:].rearrange("p j n -> p (j n)"), PS[u][:, 2 * BANK:4 * BANK]).then_inc(s["b_v"], 1)
                for u in range(G):
                    act.wait_ge(s["b_g"], now[u])
                    nc.scalar.activation(th[u], PS[u][:, 0:2 * BANK], ACT.Tanh, scale=0.5).then_inc(s["b_tanh"], 1)
                for u in range(G):
                    act.wait_ge(s["b_tqk"], now[u])
                    nc.scalar.copy(qt[u][:], bank(u, 2))
                    nc.scalar.copy(kt[u][:, 0, :], bank(u, 3)).then_inc(s["b_qkt"], 1)
                for u in range(G):
                    act.wait_ge(s["b_y"], now[u])
                    nc.scalar.activation(t2[u][:], PS[u][:, 0:2 * BANK], ACT.Square).then_inc(s["b_sq"], 1)
                for u in range(G):
                    act.wait_ge(s["b_tg"], now[u])
                    nc.scalar.copy(kt[u][:].rearrange("p k n -> p (k n)"), PS[u][:, 2 * BANK:4 * BANK]) \
                        .then_inc(s["b_gt"], 1)
                for u in range(G):
                    copy_xt(u, "ln6", 0, now[u])
                for u in range(G):
                    hidden(u, "b", now4[u])
                for u in range(G):
                    store_y(u, "b", i, now[u])

            act.wait_ge(s["b_score_c"], NB)
            act.wait_ge(s["b_x4"], NB)
            nc.scalar.activation(wcol[:], scol[:], ACT.Tanh, scale=0.5).then_inc(s["k_act"], 1)

        @block.gpsimd
        def _(pool):
            def root(u, st, now):
                pool.wait_ge(s[f"{st}_ve"], now)
                nc.gpsimd.tensor_tensor(rstd[u][:, 0:NT], ve[u][:, 0:NT], mhalf[:, 0:NT], ALU.pow) \
                    .then_inc(s[f"{st}_rstd"], 1)

            def group_root(u, a, n, now):
                pool.wait_ge(s[f"{a}_gve"], now)
                nc.gpsimd.tensor_tensor(rstd[u][:, 0:n], ve[u][:, 0:n], mhalf[:, 0:n], ALU.pow) \
                    .then_inc(s[f"{a}_grstd"], 1)

            def sum_states(u, a, n, now):
                pool.wait_ge(s[f"{a}_um"], now)
                nc.gpsimd.tensor_tensor(um[u][:, 1, 0:n], um[u][:, 1, 0:n], um[u][:, 0, 0:n], ALU.add) \
                    .then_inc(s[f"{a}_um1"], 1)
                pool.wait_ge(s[f"{a}_um1"], now)
                nc.gpsimd.tensor_tensor(um[u][:, 2, 0:n], um[u][:, 2, 0:n], um[u][:, 1, 0:n], ALU.add) \
                    .then_inc(s[f"{a}_state_sum"], 1)

            nc.gpsimd.memset(mhalf[:], -0.5).then_inc(s["w_pool"], 1)
            nc.gpsimd.memset(ones_b[:], 1.0).then_inc(s["w_pool"], 1)
            nc.gpsimd.memset(bias_f[:], 0.0).then_inc(s["w_pool"], 1)
            nc.gpsimd.memset(bias_2[:], 0.0).then_inc(s["w_pool"], 1)
            pool.wait_ge(s["w_step"], 1)
            nc.gpsimd.partition_all_reduce(amax[:, 1:2], amax[:, 0:1], P, bass.bass_isa.ReduceOp.max) \
                .then_inc(s["w_pool"], 1)
            with pool.Fori(0, NB // G) as i:
                now, past = counts(pool, i)
                for st in ("ln1", "ln2"):
                    for u in range(G):
                        root(u, st, now[u])
                for u in range(G):
                    sum_states(u, "a", P, now[u])
                for u in range(G):
                    group_root(u, "a", 4 * H0, now[u])
                for u in range(G):
                    pool.wait_ge(s["a_yn"], now[u])
                    y4 = t2[u][:, 0:S].rearrange("p (j n) -> p j n", j=NT)
                    w4 = gnw_b[:].rearrange("p (a n) -> p a n", a=1).to_broadcast((P, NT, P))
                    b4 = gnb_b[:].rearrange("p (a n) -> p a n", a=1).to_broadcast((P, NT, P))
                    nc.gpsimd.tensor_tensor(y4, y4, w4, ALU.mult).then_inc(s["a_ynw"], 1)
                    pool.wait_ge(s["a_ynw"], now[u])
                    nc.gpsimd.tensor_tensor(y4, y4, b4, ALU.add).then_inc(s["a_ynb"], 1)
                for st in ("ln3", "ln4"):
                    for u in range(G):
                        root(u, st, now[u])
            with pool.Fori(0, NB // G) as i:
                now, past = counts(pool, i)
                for u in range(G):
                    root(u, "ln5", now[u])
                for u in range(G):
                    sum_states(u, "b", VF, now[u])
                for u in range(G):
                    group_root(u, "b", 4 * H1, now[u])
                for u in range(G):
                    root(u, "ln6", now[u])

        @block.vector
        def _(dve):
            dve.sem_inc(s["xin_free"], FREE)
            dve.sem_inc(s["b_base"], FREE)

            def normalise(u, st, src, now, first_signal=None):
                for j in range(NT):
                    last = nc.vector.bn_stats(st6[u][:, j, :], src[:, j, :])
                    if j == 0 and first_signal:
                        last.then_inc(s[first_signal], 1)
                last.then_inc(s[f"{st}_stats"], 1)
                dve.wait_ge(s[f"{st}_stats"], now)
                mean_e, mean_o, m2_e, m2_o = (st6[u][:, :, k] for k in (1, 4, 2, 5))
                mean, total, diff, m2, sq = (mv[u][:, k, :] for k in range(5))
                nc.vector.tensor_tensor(total, mean_e, mean_o, ALU.add)
                nc.vector.tensor_tensor(diff, mean_e, mean_o, ALU.subtract)
                nc.vector.scalar_tensor_tensor(m2, m2_e, P * EPS, m2_o, ALU.add, ALU.add) \
                    .then_inc(s[f"{st}_mv"], 1)
                dve.wait_ge(s[f"{st}_mv"], now)
                nc.vector.scalar_tensor_tensor(sq, diff, 0.25, diff, ALU.mult, ALU.mult)
                nc.vector.tensor_scalar(mean, total, 0.5, None, ALU.mult).then_inc(s[f"{st}_sq"], 1)
                dve.wait_ge(s[f"{st}_sq"], now)
                nc.vector.scalar_tensor_tensor(ve[u][:, 0:NT], m2, 1.0 / P, sq, ALU.mult, ALU.add) \
                    .then_inc(s[f"{st}_ve"], 1)

            def apply_norm(u, st, src, now):
                dve.wait_ge(s[f"{st}_rstd"], now)
                for j in range(NT):
                    last = nc.vector.tensor_scalar(xn[u][:, j, :], src[:, j, :], mv[u][:, 0, j:j + 1],
                                                   rstd[u][:, j:j + 1], ALU.subtract, ALU.mult)
                last.then_inc(s[f"{st}_xn"], 1)

            def flat(ap):
                return ap.rearrange("p j n -> p (j n)")

            def residual(u, k, src, signal, done, now):
                dve.wait_ge(s[done], now)
                nc.vector.tensor_tensor(flat(xw[u][:]), bank(u, k), flat(src[:]), ALU.add).then_inc(s[signal], 1)
                dve.wait_ge(s[signal], now)

            def rotate(u, a, rot, now):
                dve.wait_ge(s[f"{a}_qkvg"], now)
                qk = PS[u][:, 0:2 * BANK]
                swapped = qk.rearrange("p (m e) -> p m e", e=2)[:, :, ::-1]
                nc.vector.tensor_tensor(ra[u], qk, rot[:, 0], ALU.mult)
                nc.vector.tensor_tensor(rb[u].rearrange("p (m e) -> p m e", e=2), swapped,
                                        rot[:, 1].rearrange("p (m e) -> p m e", e=2), ALU.mult) \
                    .then_inc(s[f"{a}_prod"], 1)

            def rotate_add(u, a, now):
                dve.wait_ge(s[f"{a}_prod"], now)
                nc.vector.tensor_tensor(qkr[u][:].rearrange("p q j n -> p (q j n)"), ra[u], rb[u], ALU.add).then_inc(s[f"{a}_qkr"], 1)

            def causal(u, g, h):
                m = tri[:].rearrange("p (a n) -> p a n", a=1).to_broadcast((P, NT, P))
                return nc.vector.tensor_tensor(sc[u][:, h, :].rearrange("p (j n) -> p j n", j=NT),
                                               bank(u, g).rearrange("p (j n) -> p j n", j=NT), m, ALU.mult)

            def keep_base(u, a, i, now):
                nc.vector.scalar_tensor_tensor(base[:, bass.ds((i * G + u) * S, S)], flat(xn[u][:]), 0.5,
                                               flat(xw[u][:]), ALU.mult, ALU.add).then_inc(s[f"{a}_base"], 1)
                dve.wait_ge(s[f"{a}_score"], now)
                nc.vector.tensor_copy(scol[:, bass.ds((i * G + u) * NT, NT)], bank(u, 1, 0, NT)) \
                    .then_inc(s[f"{a}_score_c"], 1)

            def combine(u, i, signal):
                for j in range(NT):
                    at = (i * G + u) * S + j * P
                    last = nc.vector.scalar_tensor_tensor(
                        xw[u][:, j, :], yall[:, bass.ds(at, P)], wcol[:, bass.ds((i * G + u) * NT + j, 1)],
                        base[:, bass.ds(at, P)], ALU.mult, ALU.add)
                last.then_inc(s[signal], 1)

            steps = [0]

            def step(ins):
                steps[0] += 1
                ins.then_inc(s["w_step"], 1)
                dve.wait_ge(s["w_step"], steps[0])

            dve.wait_ge(s["w_load"], 16 * N_LOADS)
            step(nc.vector.tensor_reduce(amax[:, 0:1], kern_s[:], AX.X, ALU.max, apply_absolute_value=True))
            dve.wait_ge(s["w_pool"], 5)
            step(nc.vector.tensor_scalar(amax[:, 2:3], amax[:, 1:2], 1.0 / 7.0, None, ALU.mult))
            step(nc.vector.reciprocal(amax[:, 3:4], amax[:, 2:3]))
            big_round = 1.5 * 2.0 ** 23
            step(nc.vector.tensor_scalar(w_ffn[:], kern_s[:], amax[:, 3:4], big_round, ALU.mult, ALU.add))
            step(nc.vector.tensor_scalar(w_ffn[:], w_ffn[:], -big_round, 7.0, ALU.add, ALU.min))
            step(nc.vector.tensor_scalar(w_ffn[:], w_ffn[:], -8.0, amax[:, 2:3], ALU.max, ALU.mult))
            dve.wait_ge(s["w_pe"], 2)
            step(nc.vector.tensor_tensor(w_ffn[:], w_ffn[:], PS[0][:, BANK:BANK + P], ALU.add))
            step(nc.vector.tensor_scalar(w_ffn[:], w_ffn[:], 0.5, None, ALU.mult))
            step(nc.vector.tensor_scalar(brow[0:1, 0, :], brow[0:1, 0, :], 0.5, None, ALU.mult))
            for n, dst in enumerate((bias_f, bias_2)):
                src = brow[0:1, n, :]
                for part in range(3):
                    row = dst[32 * part:32 * part + 1, 0, :]
                    step(nc.vector.tensor_copy(row, src))
                    if part < 2:
                        step(nc.vector.tensor_tensor(bres[0:1, n, part, :], src, row, ALU.subtract))
                        src = bres[0:1, n, part, :]
                    for j in range(1, NT):
                        step(nc.vector.tensor_copy(dst[32 * part:32 * part + 1, j, :], row))
            wv = w_qkvg[:, 2, :].rearrange("p (h e) -> p h e", h=H0)
            step(nc.vector.tensor_reduce(vmean[:], wv, AX.X, ALU.add))
            step(nc.vector.tensor_scalar(vmean[:], vmean[:], -1.0 / E0, None, ALU.mult))
            step(nc.vector.tensor_tensor(wv, wv, vmean[:].rearrange("p (h a) -> p h a", a=1)
                                         .to_broadcast((P, H0, E0)), ALU.add))
            step(nc.vector.tensor_scalar(w_o0[:], w_o0[:], 0.5, None, ALU.mult))
            step(nc.vector.tensor_scalar(w_o1[:], w_o1[:], gcol_s[:, 0:1], 0.5, ALU.mult, ALU.mult))
            step(nc.vector.tensor_copy(blkb[:], blk[:]))
            assert steps[0] == W_STEPS, steps[0]

            with dve.Fori(0, NB // G) as i:
                now, past = counts(dve, i)
                now16 = dve.snap(i * 16 + 16)
                for u in range(G):
                    dve.wait_ge(s[f"x_in{u}"], now16)
                    normalise(u, "ln1", xin[u], now[u])
                for u in range(G):
                    apply_norm(u, "ln1", xin[u], now[u])
                for u in range(G):
                    residual(u, 1, xin[u], "a_x1", "a_ffn1", now[u])
                    normalise(u, "ln2", xw[u], now[u], "xin_free")
                for u in range(G):
                    apply_norm(u, "ln2", xw[u], now[u])
                for u in range(G):
                    rotate(u, "a", rot0, now[u])
                    dve.wait_ge(s["a_tanh"], now[u])
                    nc.vector.scalar_tensor_tensor(gate[u][:, 0:S], th[u][:, 0:S], 1.0, bank(u, 3),
                                                   ALU.add, ALU.mult).then_inc(s["a_gate"], 1)
                    rotate_add(u, "a", now[u])
                for u in range(G):
                    dve.wait_ge(s["a_state"], now[u])
                    nc.vector.tensor_tensor(um[u][:, :, 0:P], bank(u, 2, 0, 3 * P).rearrange("p (c n) -> p c n", c=3),
                                            bd0[:].rearrange("p (a n) -> p a n", a=1).to_broadcast((P, 3, P)),
                                            ALU.mult).then_inc(s["a_um"], 1)
                for parity, name in ((0, "e"), (1, "o")):
                    for u in range(G):
                        dve.wait_ge(s[f"a_sc_{name}"], now[u])
                        for g in range(4):
                            last = causal(u, g, 2 * g + parity)
                        last.then_inc(s[f"a_msk_{name}"], 1)
                for u in range(G):
                    dve.wait_ge(s["a_sq"], now[u])
                    nc.vector.tensor_reduce(ve[u][:, 0:4 * H0], t2[u][:, S:2 * S].rearrange("p (h e) -> p h e", e=E0),
                                            AX.X, ALU.add).then_inc(s["a_var"], 1)
                    dve.wait_ge(s["a_var"], now[u])
                    nc.vector.tensor_scalar(ve[u][:, 0:4 * H0], ve[u][:, 0:4 * H0], 1.0 / E0, EPS, ALU.mult, ALU.add) \
                        .then_inc(s["a_gve"], 1)
                for u in range(G):
                    dve.wait_ge(s["a_grstd"], now[u])
                    nc.vector.tensor_tensor(t2[u][:, 0:S].rearrange("p (h e) -> p h e", e=E0),
                                            bank(u, 0).rearrange("p (h e) -> p h e", e=E0),
                                            rstd[u][:, 0:4 * H0].rearrange("p (h a) -> p h a", a=1)
                                            .to_broadcast((P, 4 * H0, E0)), ALU.mult).then_inc(s["a_yn"], 1)
                for u in range(G):
                    dve.wait_ge(s["a_ynb"], now[u])
                    nc.vector.tensor_tensor(t2[u][:, 0:S], t2[u][:, 0:S], gate[u][:, 0:S], ALU.mult) \
                        .then_inc(s["a_gy"], 1)
                for u in range(G):
                    residual(u, 2, xw[u], "a_x2", "a_wo", now[u])
                    normalise(u, "ln3", xw[u], now[u])
                for u in range(G):
                    apply_norm(u, "ln3", xw[u], now[u])
                for u in range(G):
                    residual(u, 1, xw[u], "a_x3", "a_ffn3", now[u])
                    normalise(u, "ln4", xw[u], now[u])
                for u in range(G):
                    apply_norm(u, "ln4", xw[u], now[u])
                for u in range(G):
                    dve.wait_ge(s["ln4_xn"], now[u])
                    keep_base(u, "a", i, now[u])

            def topk(n0, x_used, act_done):
                n = [n0]

                def step(ins):
                    n[0] += 1
                    ins.then_inc(s["k_dve"], 1)
                    dve.wait_ge(s["k_dve"], n[0])

                dve.wait_ge(s[x_used], NB)
                dve.wait_ge(s["a_ystore" if not n0 else "b_ystore"], NB + FREE)
                step(nc.vector.tensor_copy(srep, scol[:].rearrange("p (b j a) -> p j b a", j=NT, a=1)
                                           .to_broadcast((P, NT, NB, REP))))
                pes = (ROUNDS + 2) * (n0 // K_STEPS)
                dve.wait_ge(s["k_pe"], pes + 1)
                step(nc.vector.tensor_copy(srow, PS[0][:, 0:S]))
                step(nc.vector.tensor_reduce(amax[:, 0:1], srow, AX.X, ALU.max, apply_absolute_value=True))
                step(nc.vector.tensor_scalar(amax[:, 0:1], amax[:, 0:1], 1e-30, None, ALU.max))
                step(nc.vector.tensor_scalar(amax[:, 1:2].bitcast(I32), amax[:, 0:1].bitcast(I32), 0x7f800000, None,
                                             ALU.bitwise_and))
                step(nc.vector.tensor_scalar(amax[:, 1:2], amax[:, 1:2], 2.0, None, ALU.mult))
                step(nc.vector.reciprocal(amax[:, 2:3], amax[:, 1:2]))
                step(nc.vector.tensor_scalar(srow, srow, amax[:, 2:3], None, ALU.mult))
                step(nc.vector.memset(zero, 0.0))
                lo, hi, thr, cnt = amax[:, 0:1], amax[:, 1:2], amax[:, 2:3], amax[:, 3:4]
                step(nc.vector.memset(lo, -1.0))
                assert n[0] - n0 == K_HEAD
                for r in range(ROUNDS):
                    width = 2.0 / REP ** (r + 1)
                    step(nc.vector.tensor_tensor(thr, rs[:, r:r + 1], lo, ALU.add))
                    step(nc.vector.tensor_scalar(msk_a, srow, thr, None, ALU.is_ge, ALU.add, accum_out=cnt))
                    step(nc.vector.tensor_scalar(rankb.bitcast(BF16)[:, 0:1], cnt, float(TOPK), None, ALU.is_ge))
                    dve.wait_ge(s["k_pe"], pes + r + 2)
                    if r == ROUNDS - 1:
                        step(nc.vector.tensor_scalar(hi, PS[0][:, BANK:BANK + 1], 1.0, width, ALU.add, ALU.mult))
                        step(nc.vector.tensor_tensor(hi, hi, lo, ALU.add))
                    step(nc.vector.scalar_tensor_tensor(lo, PS[0][:, BANK:BANK + 1], width, lo, ALU.mult, ALU.add))
                step(nc.vector.tensor_scalar(msk_a, srow, hi, None, ALU.is_ge, ALU.add, accum_out=cnt))
                step(nc.vector.scalar_tensor_tensor(msk_b, srow, lo, msk_a, ALU.is_ge, ALU.subtract))
                step(nc.vector.tensor_scalar(cnt, cnt, -1.0, float(TOPK), ALU.mult, ALU.add))
                step(nc.vector.tensor_tensor_scan(pre, msk_b, zero, 0.0, ALU.add, ALU.add))
                step(nc.vector.scalar_tensor_tensor(pre, pre, cnt, msk_b, ALU.is_le, ALU.mult))
                step(nc.vector.tensor_tensor(msk_a, msk_a, pre, ALU.add))
                dve.wait_ge(s["k_act"], act_done)
                step(nc.vector.tensor_scalar(wcol[:], wcol[:], 1.0, 0.25, ALU.add, ALU.mult))
                dve.wait_ge(s["k_pe"], pes + ROUNDS + 2)
                w3 = wcol[:].rearrange("p (b j) -> p j b", j=NT)
                m3 = PS[0][:, 0:S].rearrange("p (j b r) -> p j b r", j=NT, b=NB)[:, :, :, 0]
                step(nc.vector.tensor_tensor(w3, m3, w3, ALU.mult))
                assert n[0] - n0 == K_STEPS, n[0] - n0

            topk(0, "a_score_c", 1)

            with dve.Fori(0, NB // G) as i:
                now, past = counts(dve, i)
                for u in range(G):
                    dve.wait_ge(s["b_base"], past)
                    combine(u, i, "b_x4")
                    dve.wait_ge(s["b_x4"], now[u])
                    normalise(u, "ln5", xw[u], now[u])
                for u in range(G):
                    apply_norm(u, "ln5", xw[u], now[u])
                for u in range(G):
                    rotate(u, "b", rot1, now[u])
                    rotate_add(u, "b", now[u])
                for u in range(G):
                    dve.wait_ge(s["b_tanh"], now[u])
                    nc.vector.scalar_tensor_tensor(gate[u][:], th[u], 1.0, PS[u][:, 0:2 * BANK],
                                                   ALU.add, ALU.mult).then_inc(s["b_gate"], 1)
                for u in range(G):
                    dve.wait_ge(s["b_state"], now[u])
                    nc.vector.tensor_tensor(um[u][:], PS[u][:, 0:3 * VF].rearrange("p (c n) -> p c n", c=3),
                                            bd1[:].rearrange("p (a n) -> p a n", a=1).to_broadcast((P, 3, VF)),
                                            ALU.mult).then_inc(s["b_um"], 1)
                for u in range(G):
                    dve.wait_ge(s["b_sc"], now[u])
                    for g in range(H1):
                        last = causal(u, g, g)
                    last.then_inc(s["b_msk"], 1)
                for u in range(G):
                    dve.wait_ge(s["b_sq"], now[u])
                    nc.vector.tensor_reduce(ve[u][:, 0:4 * H1], t2[u][:].rearrange("p (h e) -> p h e", e=V1),
                                            AX.X, ALU.add).then_inc(s["b_var"], 1)
                    dve.wait_ge(s["b_var"], now[u])
                    nc.vector.tensor_scalar(ve[u][:, 0:4 * H1], ve[u][:, 0:4 * H1], 1.0 / V1, EPS, ALU.mult, ALU.add) \
                        .then_inc(s["b_gve"], 1)
                for u in range(G):
                    dve.wait_ge(s["b_grstd"], now[u])
                    nc.vector.tensor_tensor(t2[u][:].rearrange("p (h e) -> p h e", e=V1),
                                            PS[u][:, 0:2 * BANK].rearrange("p (h e) -> p h e", e=V1),
                                            rstd[u][:, 0:4 * H1].rearrange("p (h a) -> p h a", a=1)
                                            .to_broadcast((P, 4 * H1, V1)), ALU.mult).then_inc(s["b_yn"], 1)
                    dve.wait_ge(s["b_yn"], now[u])
                    nc.vector.tensor_tensor(t2[u][:], t2[u][:], gate[u][:], ALU.mult).then_inc(s["b_gy"], 1)
                for u in range(G):
                    residual(u, 0, xw[u], "b_x5", "b_wo", now[u])
                    normalise(u, "ln6", xw[u], now[u])
                for u in range(G):
                    apply_norm(u, "ln6", xw[u], now[u])
                for u in range(G):
                    dve.wait_ge(s["ln6_xn"], now[u])
                    keep_base(u, "b", i, now[u])

            topk(K_STEPS, "b_score_c", 2)
            dve.wait_ge(s["b_base"], NB + FREE)

            with dve.Fori(0, NB // G) as i:
                past16 = dve.snap(i * (16 * G) + FREE)
                for u in range(G):
                    dve.wait_ge(s["c_store"], past16)
                    combine(u, i, "c_out")


FREE = 1
W_STEPS = 8 + 1 + 2 * (3 + 2 + 9) + 3 + 3
W_POOL = 5
K_HEAD, K_ROUND = 10, 4
K_STEPS = K_HEAD + ROUNDS * K_ROUND + 2 + 8


def tables():
    f = np.float32
    pos = np.arange(S, dtype=f)

    def lay(t):
        return t.reshape(NT, P, -1).transpose(1, 0, 2)

    def signed(sin):
        out = np.repeat(sin, 2, axis=-1)
        out[..., 0::2] *= -1
        return out

    half = E0 // 2
    vec = ((np.arange(0, E0, 2, dtype=f) + f(0.4 * E0)) / f(1.4 * E0)).astype(np.float64)
    inv = f(1) / (f(10000) ** (np.arange(half, dtype=f) / f(half)))
    ang = (pos[:, None] * inv[None, :]).astype(np.float64)
    gam = (f(1) - np.exp(np.linspace(np.log(1 / 32), np.log(1 / 64), H0).astype(f))).astype(np.float64)
    mid = pos.astype(np.float64) - S / 2
    r0 = np.zeros((2, S, 2, H0, E0))
    for q, sign in ((0, 1.0), (1, -1.0)):
        size = vec[None, None, :] ** (sign * mid[:, None, None] / 64) * gam[None, :, None] ** (sign * mid[:, None, None])
        r0[0, :, q] = np.repeat(np.cos(ang)[:, None, :] * size, 2, axis=-1)
        r0[1, :, q] = signed(np.sin(ang)[:, None, :] * size)
    inv = f(1) / (f(10000) ** (np.arange(0, K1, 2, dtype=f) / f(K1)))
    ang = (pos[:, None] * inv[None, :]).astype(np.float64)
    gam = 1.0 - 2.0 ** (-5.0 - np.arange(H1))
    r1 = np.zeros((2, S, 2, H1, K1))
    for q, sign in ((0, 1.0), (1, -1.0)):
        size = gam[None, :, None] ** (sign * mid[:, None, None]) * (K1 ** -0.5 if q == 0 else 1.0)
        r1[0, :, q] = np.repeat(np.cos(ang)[:, None, :] * size, 2, axis=-1)
        r1[1, :, q] = signed(np.sin(ang)[:, None, :] * size)

    def rot(r):
        return np.stack([lay(r[a, :, q].reshape(S, P)) for a in range(2) for q in range(2)], axis=1).reshape(P, -1).astype(f)

    i = np.arange(P)
    return {
        "ident": np.eye(P, dtype=f),
        "tri": (i[:, None] <= i[None, :]).astype(f),
        "bd0": (i[:, None] // E0 == i[None, :] // E0).astype(f),
        "bd1": (i[:, None] // K1 == np.arange(VF)[None, :] // V1).astype(f),
        "par": np.stack([(i // E0) % 2 == 0, (i // E0) % 2 == 1], axis=1).astype(f),
        "rot0": rot(r0), "rot1": rot(r1),
        "blk": (i[:, None] // REP == i[None, :] // REP).astype(f),
        "rs": ((i % REP + 1)[:, None] * 2.0 / REP ** np.arange(1, ROUNDS + 1)[None, :]).astype(f),
    }


def kernel(**inputs):
    import concourse.bacc as _bacc
    from concourse.bass_utils import run_bass_kernel_spmd as _run

    a = {k: np.ascontiguousarray(v) for k, v in inputs.items()}

    def paired(w):
        return np.ascontiguousarray(w.reshape(H1, 2, K1 // 2, P).transpose(3, 0, 2, 1).reshape(P, P))

    arrays = {
        "x": a["L0_attn_X"], "wq0": a["L0_attn_W_Q"], "wk0": a["L0_attn_W_K"], "wv0": a["L0_attn_W_V"],
        "wg0": a["L0_attn_W_G"], "wo0": a["L0_attn_W_O"], "gnw": a["L0_attn_gn_weight"], "gnb": a["L0_attn_gn_bias"],
        "kern": a["L0_ffn_kernel"], "bias": a["L0_ffn_bias"], "fa": a["L0_ffn_a"], "fb": a["L0_ffn_b"],
        "wq1": paired(a["L1_attn_Wq"]), "wk1": paired(a["L1_attn_Wk"]),
        "wv1": np.ascontiguousarray(a["L1_attn_Wv"].T), "wg1": np.ascontiguousarray(a["L1_attn_Wg"].T),
        "wo1": np.ascontiguousarray(a["L1_attn_Wo"].T),
        "gcol": np.ascontiguousarray(np.tile(a["L1_attn_gnorm_w"], P // V1).reshape(P, 1)),
        "wr": a["L1_ffn_w_router"], "w1": a["L1_ffn_W1"], "b1": a["L1_ffn_b1"], "w2": a["L1_ffn_W2"],
        "b2": a["L1_ffn_b2"], **tables(),
    }
    nc = _bacc.Bacc("TRN2", target_bir_lowering=False, num_devices=1)
    maps, args = {}, []
    for name, v in arrays.items():
        maps[f"in_{name}"] = v
        args.append(nc.dram_tensor(f"in_{name}", v.shape, mybir.dt.from_np(v.dtype), kind="ExternalInput").ap())
    args.append(nc.dram_tensor("out_x", a["L0_attn_X"].shape, F32, kind="ExternalOutput").ap())
    program(nc, *args)
    r = _run(nc, [maps], core_ids=[0])
    return r.results[0]["out_x"]
```

```python
from contextlib import ExitStack

import numpy as np

import concourse.bass as bass
from concourse import mybir

ALU = mybir.AluOpType
ACT = mybir.ActivationFunctionType
AX = mybir.AxisListType
F32 = mybir.dt.float32
BF16 = mybir.dt.bfloat16
I32 = mybir.dt.int32

P = 128
NB, NT = 16, 4
S = NT * P
EPS = 1e-5
H0, E0 = 8, 16
H1, K1, V1 = 4, 32, 64
VF = H1 * V1
FH = 512
NF = FH // P
TOPK = S // 2
REP, ROUNDS = 8, 8
BANK = 512
ACT_HEADS = 5
BK = 96

LN_STEPS = ("stats", "mv", "sq", "ve", "rstd", "xn", "t", "xt")
X0, X1, X2 = 5, 6, 7


class Slot:

    def __init__(self, k, counts, parity, loads=None):
        self.k, self.counts, self.parity = k, counts, parity
        self.loads = loads

    def count(self, d):
        return self.counts[d + 2]

    def batch(self, d):
        return self.k + d

    def buf(self, d):
        return (self.parity + d) % 2


def run_slots(eng, slot, start, loads=False):
    def peeled(k):
        slot(Slot(k, [start + k + d + 1 for d in range(-2, 3)], k % 2, 16 * ((k + 2) // 2 + 1)),
             prepare=k + 1 < NB, score=0 <= k < NB, complete=k >= 1)
    for k in (-1, 0, 1):
        peeled(k)
    with eng.Fori(0, (NB - 4) // 2) as i:
        for j in range(2):
            k = 2 + j
            counts = [eng.snap(i * 2 + (start + k + d + 1)) for d in range(-2, 3)]
            landed = eng.snap(i * 16 + 16 * ((k + 2) // 2 + 1)) if loads else None
            slot(Slot(i * 2 + k, counts, j, landed), prepare=True, score=True, complete=True)
    for k in (NB - 2, NB - 1, NB):
        peeled(k)


def program(nc, x, wq0, wk0, wv0, wg0, wo0, gnw, gnb, kern, bias, fa, fb,
            wq1, wk1, wv1, wg1, wo1, gcol, wr, w1, b1, w2, b2,
            ident_d, tri_d, bd0_d, bd1_d, hm_d, rot0_d, rot1_d, blk_d, rs_d, out):
    with ExitStack() as ctx:
        def sb(name, shape, dt=F32):
            return ctx.enter_context(nc.sbuf_tensor(name, shape, dt))

        def sem(name):
            return ctx.enter_context(nc.semaphore(name))

        ident = sb("ident", [P, P])
        tri = sb("tri", [P, P])
        bd0 = sb("bd0", [P, P])
        bd1 = sb("bd1", [P, VF])
        hm = sb("hm", [P, H0 + H1])
        rot = sb("rot", [P, 2, 2 * S])
        rs = sb("rs", [P, ROUNDS])
        blkb = sb("blkb", [P, P], BF16)
        ones_b = sb("ones_b", [BK, P], BF16)
        w_qkvg = sb("w_qkvg", [P, 4, P])
        w_o0 = sb("w_o0", [P, P])
        gnw_b = sb("gnw_b", [P, P])
        gnb_b = sb("gnb_b", [P, P])
        amax = sb("amax", [P, 4])
        vmean = sb("vmean", [P, H0])
        w_ffn = sb("w_ffn", [P, P])
        bias_f = sb("bias_f", [BK, NT, P], BF16)
        bias_2 = sb("bias_2", [BK, NT, P], BF16)
        w_qkv1 = sb("w_qkv1", [P, 2 * P + VF])
        w_g1 = sb("w_g1", [P, VF])
        w_o1 = sb("w_o1", [P, 2, P])
        gcol_s = sb("gcol_s", [P, 1])
        wr_b = sb("wr_b", [P, P])
        w1_s = sb("w1_s", [P, NF, P])
        b1_s = sb("b1_s", [P, NF])
        w2_s = sb("w2_s", [P, NF, P])
        mhalf = sb("mhalf", [P, 4 * H0])

        base = sb("base", [P, NB * S])
        yall = sb("yall", [P, NB * S])
        scol = sb("scol", [P, NB * NT])
        wcol = sb("wcol", [P, NB * NT])

        xin = [sb(f"xin{p}", [P, NT, P]) for p in range(2)]
        x1 = [sb(f"x1_{p}", [P, NT, P]) for p in range(2)]
        gate = [sb(f"gate{p}", [P, NT * VF]) for p in range(2)]
        x2 = sb("x2", [P, NT, P])
        xn = {n: sb(f"xn_{n}", [P, NT, P]) for n in "pc"}
        st6 = {n: sb(f"st6_{n}", [P, NT, 6]) for n in "pc"}
        mv = {n: sb(f"mv_{n}", [P, 5, NT]) for n in "pc"}
        ve = {n: sb(f"ve_{n}", [P, NT]) for n in "pc"}
        rstd = {n: sb(f"rstd_{n}", [P, NT]) for n in "pc"}
        xt = {n: sb(f"xt_{n}", [P, NT, P]) for n in ("p", "c", "r")}
        qkr = sb("qkr", [P, 2, NT, P])
        ra = sb("ra", [P, 2 * S])
        rb = sb("rb", [P, 2 * S])
        vv = sb("vv", [P, NT, VF])
        qt = sb("qt", [P, S])
        kt = sb("kt", [P, S])
        qm = sb("qm", [P, NT * H0 * P])
        vm = sb("vm", [P, NT * H0 * P])
        sc = [sb(f"sc{p}", [P, H0 * P]) for p in range(2)]
        um = sb("um", [P, 3, VF])
        gve = sb("gve", [P, 4 * H0])
        grstd = sb("grstd", [P, 4 * H0])
        sq = sb("sq", [P, NT * VF])
        t2 = sb("t2", [P, NT * VF])
        rp = sb("rp", [P, NT, P])
        gt = sb("gt", [P, 2, S])
        hid = sb("hid", [P, NF, S])
        th = hid[:].rearrange("p f n -> p (f n)")[:, 2 * S:4 * S]
        PS = ctx.enter_context(nc.psum_tensor("ps", [P, 8 * BANK], F32))

        def bank(k, a=0, n=BANK):
            return PS[:, k * BANK + a:k * BANK + a + n]

        kern_s, fb_s, faT = ra[:, 0:P], ra[0:16, P:2 * P], ra[0:16, 2 * P:3 * P]
        fa_s, blk = ra[:, 3 * P:3 * P + 16], ra[:, 4 * P:5 * P]
        brow = rb[0:1, 0:2 * P].rearrange("p (a n) -> p a n", a=2)
        bres = rb[0:1, 2 * P:6 * P].rearrange("p (a b n) -> p a b n", a=2, b=2)
        srow, msk_a, msk_b, pre, zero, srep_f = (qm[:, k * S:(k + 1) * S] for k in range(6))
        rankb = qm[:, 6 * S:6 * S + 1]
        srep = srep_f.rearrange("p (j b r) -> p j b r", j=NT, b=NB)

        names = [f"{st}_{k}" for st in ("ln_f1", "ln_ret", "ln_f2", "ln_mod") for k in LN_STEPS]
        names += [f"{k}{c}" for k in ("sc", "msk", "h", "act") for c in range(4)]
        names += ["ffn1", "x1", "qk", "v_mm", "vv", "g_mm", "prod", "qkr", "v", "tanh", "gate", "tqk", "qm", "state",
                  "um", "um1", "state_sum", "av0", "av1", "av2", "y", "sq", "var", "gve", "grstd", "yn", "ynw", "ynb",
                  "gy", "tg", "gt", "wo", "x2", "ffn2", "x3", "rprod", "score", "mod", "ystore", "base"]
        names += ["qt", "qm_dve"]
        names += ["x_in0", "x_in1", "out_dve", "weighted", "out_pool", "store", "rot_in", "w_load", "w_late", "w_step",
                  "w_pool", "w_pe", "w_act", "vm_zero", "k_dve", "k_pe", "k_act"]
        s = {n: sem(n) for n in names}

        def wait(eng, name, count):
            if not isinstance(count, int) or count > 0:
                eng.wait_ge(s[name], count)

        block = ctx.enter_context(nc.Block())

        @block.sync
        def _(sp):
            def load_x(b, p):
                sp.dma_start(xin[p][:], x[bass.ds(b, 1)].rearrange("a (j p) n -> (a p) j n", p=P)) \
                    .then_inc(s[f"x_in{p}"], 16)

            def load(dst, src):
                sp.dma_start(dst, src).then_inc(s["w_load"], 16)
            load_x(0, 0)
            load_x(1, 1)
            def load_late(dst, src):
                sp.dma_start(dst, src).then_inc(s["w_late"], 16)
            with nc.allow_non_contiguous_dma("weights, once"):
                load(kern_s, kern)
                load(fa_s, fa)
                load(fb_s, fb)
                load(ident[:], ident_d)
                load(brow[0:1, 0, :], bias.rearrange("(a n) -> a n", a=1))
                load(brow[0:1, 1, :], b2.rearrange("(a n) -> a n", a=1))
                for n, w in enumerate((wq0, wk0, wv0)):
                    load(w_qkvg[:, n, :].rearrange("p (h e) -> p h e", h=H0), w.rearrange("h p e -> p h e"))
                load(w_o0[:], wo0)
                load(blk, blk_d)
                load_late(w_qkvg[:, 3, :], wg0)
                load_late(gnw_b[:], gnw.rearrange("(a n) -> a n", a=1).to_broadcast((P, P)))
                load_late(gnb_b[:], gnb.rearrange("(a n) -> a n", a=1).to_broadcast((P, P)))
                load_late(w_qkv1[:, 0:P], wq1)
                load_late(w_qkv1[:, P:2 * P], wk1)
                load_late(w_qkv1[:, 2 * P:], wv1)
                load_late(w_g1[:], wg1)
                load_late(tri[:], tri_d)
                load_late(bd0[:], bd0_d)
                load_late(bd1[:], bd1_d)
                load_late(hm[:], hm_d)
                load_late(rot[:].rearrange("p a n -> p (a n)"), rot0_d)
                load_late(rs[:], rs_d)

            with sp.Fori(0, NB // 2 - 1) as i:
                for p in range(2):
                    sp.wait_ge(s["x1"], sp.snap(i * 2 + (p + 1)))
                    load_x(i * 2 + (p + 2), p)

            sp.wait_ge(s["prod"], NB)
            sp.dma_start(rot[:].rearrange("p a n -> p (a n)"), rot1_d).then_inc(s["rot_in"], 16)

            def store_x(b):
                sp.dma_start(out[bass.ds(b, 1)].rearrange("a (j p) n -> (a p) j n", p=P),
                             base[:, bass.ds(b * S, S)].rearrange("p (j n) -> p j n", j=NT)).then_inc(s["store"], 16)

            with sp.Fori(0, NB // 2) as i:
                n = sp.snap(i + 1)
                sp.wait_ge(s["out_dve"], n)
                store_x(i * 2)
                sp.wait_ge(s["out_pool"], n)
                store_x(i * 2 + 1)
            sp.wait_ge(s["store"], 16 * NB)

        N_LOADS = 13
        N_LATE = 17

        @block.tensor
        def _(pe):
            def transpose4(st, src, k, count):
                wait(pe, f"{st}_xn", count)
                for j in range(NT):
                    mm = nc.tensor.transpose(bank(k, j * P, P), src[:, j, :], ident[:])
                mm.then_inc(s[f"{st}_t"], 1)

            def tilewise(out_at, xt_src, w, signal=None):
                for j in range(NT):
                    mm = nc.tensor.matmul(out_at(j), xt_src[:, j, :], w, start=True, stop=True,
                                          skip_group_check=True)
                if signal:
                    mm.then_inc(s[signal], 1)

            def ffn(st, src, k, count, signal):
                wait(pe, f"{st}_xt", count)
                nc.tensor.matmul(bank(k), ones_b[:], bias_f[:].rearrange("p j n -> p (j n)"),
                                 start=True, stop=False, skip_group_check=True)
                for j in range(NT):
                    mm = nc.tensor.matmul(bank(k, j * P, P), src[:, j, :], w_ffn[:],
                                          start=False, stop=(j == NT - 1), skip_group_check=True)
                mm.then_inc(s[signal], 1)

            def project(k, w, signal=None):
                tilewise(lambda j: bank(k, j * P, P), xt["p"], w, signal)

            def transpose_qk(k, count):
                wait(pe, "qkr", count)
                for q in range(2):
                    for j in range(NT):
                        mm = nc.tensor.transpose(bank(k + q, j * P, P), qkr[:, q, j, :], ident[:])
                mm.then_inc(s["tqk"], 1)

            def states(k, width):
                for c in range(NT - 1):
                    mm = nc.tensor.matmul(bank(k, c * width, width), qkr[:, 1, c, :], vv[:, c, 0:width],
                                          start=True, stop=True, skip_group_check=True)
                mm.then_inc(s["state"], 1)

            def scores(c, k, heads):
                for g in range(heads // 4):
                    mm = nc.tensor.matmul(bank(k + g), kt[:, c * P:(c + 1) * P],
                                          qm[:, (c * heads + 4 * g) * P:(c * heads + 4 * g + 4) * P],
                                          start=True, stop=True)
                mm.then_inc(s[f"sc{c}"], 1)

            def attend(a, c, sl, heads):
                wait(pe, f"msk{c}", sl.count(0))
                if c == 1:
                    wait(pe, "state_sum", sl.count(0))
                width = P if a == "a" else VF
                at = 4 * BANK + c * P if a == "a" else 3 * BANK + c * VF
                if c:
                    nc.tensor.matmul(PS[:, at:at + width], qt[:, c * P:(c + 1) * P], um[:, c - 1, 0:width],
                                     start=True, stop=False, skip_group_check=True)
                for h in range(heads):
                    off = at + (h // 2 * P if a == "b" else 0)
                    mm = nc.tensor.matmul(PS[:, off:off + P], sc[c % 2][:, h * P:(h + 1) * P],
                                          vm[:, (c * heads + h) * P:(c * heads + h + 1) * P],
                                          start=(c == 0 and h == 0), stop=(h == heads - 1),
                                          skip_group_check=True)
                mm.then_inc(s["y"] if c == NT - 1 else s[f"av{c}"], 1)

            def routed_up(f, k):
                nc.tensor.matmul(bank(k), w1_s[:, f, :], xt["r"][:].rearrange("p j n -> p (j n)"),
                                 start=True, stop=True).then_inc(s[f"h{f}"], 1)

            def routed_down(f, count):
                wait(pe, f"act{f}", count)
                if f == 0:
                    nc.tensor.matmul(bank(X0), ones_b[:], bias_2[:].rearrange("p j n -> p (j n)"),
                                     start=True, stop=False, skip_group_check=True)
                for j in range(NT):
                    mm = nc.tensor.matmul(bank(X0, j * P, P), hid[:, f, j * P:(j + 1) * P],
                                          w2_s[:, f, :], start=False, stop=(f == NF - 1 and j == NT - 1),
                                          skip_group_check=True)
                if f == NF - 1:
                    mm.then_inc(s["mod"], 1)

            pe.wait_ge(s["w_load"], 16 * N_LOADS)
            nc.tensor.transpose(PS[0:16, 0:P], fa_s, ident[:]).then_inc(s["w_pe"], 1)
            pe.wait_ge(s["w_act"], 1)
            nc.tensor.matmul(bank(1, 0, P), faT, fb_s, start=True, stop=True).then_inc(s["w_pe"], 1)
            pe.wait_ge(s["w_late"], 16 * N_LATE)
            pe.wait_ge(s["w_step"], W_STEPS)
            pe.wait_ge(s["w_pool"], W_POOL)

            def score_rows(n0):
                pe.wait_ge(s["k_dve"], n0 + 2)
                for j in range(NT):
                    mm = nc.tensor.transpose(bank(2, j * P, P), srep_f[:, j * P:(j + 1) * P], ident[:])
                mm.then_inc(s["k_pe"], 1)

            def slot_a(sl, prepare, score, complete):
                now, new, old = sl.count(0), sl.count(1), sl.count(-1)
                if score:
                    wait(pe, "qm", now)
                    wait(pe, "qm_dve", now)
                    scores(0, 0, H0)
                if prepare:
                    wait(pe, "ystore", sl.count(-2))
                    transpose4("ln_f1", xn["p"], X0, new)
                if score:
                    wait(pe, "um", now)
                    scores(1, 2, H0)
                if complete:
                    wait(pe, "gy", old)
                    for j in range(NT):
                        mm = nc.tensor.transpose(bank(X1, j * P, P), t2[:, j * P:(j + 1) * P], ident[:])
                    mm.then_inc(s["tg"], 1)
                if prepare:
                    ffn("ln_f1", xt["p"], X2, new, "ffn1")
                if complete:
                    wait(pe, "gt", old)
                    tilewise(lambda j: bank(X0, j * P, P), gt[:, 0, :].rearrange("p (j n) -> p j n", j=NT), w_o0[:],
                             "wo")
                if score:
                    attend("a", 0, sl, H0)
                    scores(2, 0, H0)
                    attend("a", 1, sl, H0)
                if prepare:
                    transpose4("ln_ret", xn["p"], X1, new)
                if score:
                    scores(3, 2, H0)
                if prepare:
                    wait(pe, "ln_ret_xt", new)
                    project(X1, w_qkvg[:, 0, :])
                if complete:
                    transpose4("ln_f2", xn["c"], X0, old)
                if prepare:
                    project(X2, w_qkvg[:, 1, :], "qk")
                if complete:
                    ffn("ln_f2", xt["c"], X0, old, "ffn2")
                if score:
                    wait(pe, "msk2", now)
                if prepare:
                    for n in range(2):
                        tilewise(lambda j: bank(n, j * P, P), xt["p"], w_qkvg[:, 2 + n, :],
                                 "g_mm" if n else "v_mm")
                if score:
                    attend("a", 2, sl, H0)
                    attend("a", 3, sl, H0)
                if prepare:
                    transpose_qk(X1, new)
                if complete:
                    transpose4("ln_mod", xn["c"], X0, old)
                if prepare:
                    wait(pe, "vv", new)
                    states(2, P)
                if prepare and not complete:
                    wait(pe, "v", new)
                    wait(pe, "gate", new)
                if complete:
                    wait(pe, "ln_mod_xt", old)
                    for f, k in enumerate((3, 0, 1, 3)):
                        if f == 1 and prepare:
                            wait(pe, "v", new)
                        if f == 2 and prepare:
                            wait(pe, "gate", new)
                        if f == 3:
                            wait(pe, "act0", old)
                        routed_up(f, k)
                    if not score:
                        score_rows(0)
                    for f in range(NF):
                        routed_down(f, old)

            def slot_b(sl, prepare, score, complete):
                now, new, old = sl.count(0), sl.count(1), sl.count(-1)
                if score:
                    wait(pe, "qm", now)
                    scores(0, 0, H1)
                    scores(1, 1, H1)
                if prepare:
                    wait(pe, "ystore", sl.count(-2))
                    transpose4("ln_ret", xn["p"], X0, new)
                if complete:
                    wait(pe, "gy", old)
                    if score:
                        wait(pe, "um", now)
                    for k in range(2):
                        for j in range(NT):
                            mm = nc.tensor.transpose(bank(X1 + k, j * P, P),
                                                     t2[:, j * VF + k * P:j * VF + (k + 1) * P], ident[:])
                    mm.then_inc(s["tg"], 1)
                if score:
                    attend("b", 0, sl, H1)
                    scores(2, 2, H1)
                    attend("b", 1, sl, H1)
                if complete:
                    if prepare:
                        wait(pe, "ln_ret_xt", new)
                    else:
                        wait(pe, "ystore", sl.count(-2))
                    wait(pe, "gt", old)
                    for j in range(NT):
                        for k in range(2):
                            mm = nc.tensor.matmul(bank(X0, j * P, P), gt[:, k, j * P:(j + 1) * P], w_o1[:, k, :],
                                                  start=(k == 0), stop=(k == 1), skip_group_check=True)
                    mm.then_inc(s["wo"], 1)
                if prepare:
                    wait(pe, "ln_ret_xt", new)
                    if score and not complete:
                        wait(pe, "um", now)
                    project(X1, w_qkv1[:, 0:P])
                    project(X2, w_qkv1[:, P:2 * P], "qk")
                if score:
                    wait(pe, "msk2", now)
                    scores(3, 2, H1)
                if prepare:
                    tilewise(lambda j: bank(j // 2, (j % 2) * VF, VF), xt["p"], w_qkv1[:, 2 * P:], "v_mm")
                if score:
                    attend("b", 2, sl, H1)
                    attend("b", 3, sl, H1)
                if prepare:
                    wait(pe, "prod", new)
                    tilewise(lambda j: bank(X1 + j // 2, (j % 2) * VF, VF), xt["p"], w_g1[:], "g_mm")
                if complete:
                    transpose4("ln_mod", xn["c"], X0, old)
                if prepare:
                    wait(pe, "v", new)
                    transpose_qk(1, new)
                if complete:
                    wait(pe, "ln_mod_xt", old)
                    routed_up(0, 0)
                if prepare:
                    wait(pe, "gate", new)
                if complete:
                    routed_up(1, X1)
                    routed_up(2, X2)
                    wait(pe, "act0", old)
                    routed_up(3, 0)
                    if not score:
                        score_rows(K_STEPS)
                    for f in range(3):
                        routed_down(f, old)
                if prepare:
                    states(X1, VF)
                if complete:
                    routed_down(3, old)

            def topk(n0):
                for r in range(ROUNDS):
                    pe.wait_ge(s["k_dve"], n0 + K_HEAD + K_ROUND * r + K_ROUND - 1)
                    nc.tensor.matmul(bank(4, 0, 1), blkb[:], rankb.bitcast(BF16)[:, 0:1],
                                     start=True, stop=True).then_inc(s["k_pe"], 1)
                pe.wait_ge(s["k_dve"], n0 + K_STEPS - 1)
                for j in range(NT):
                    mm = nc.tensor.transpose(bank(2, j * P, P), msk_a[:, j * P:(j + 1) * P], ident[:])
                mm.then_inc(s["k_pe"], 1)

            run_slots(pe, slot_a, 0)
            topk(0)
            pe.wait_ge(s["k_dve"], K_STEPS)
            run_slots(pe, slot_b, NB)
            topk(K_STEPS)

        @block.scalar
        def _(act):
            def copy_xt(st, dst, k, count):
                wait(act, f"{st}_t", count)
                nc.scalar.copy(dst[:].rearrange("p j n -> p (j n)"), bank(k)).then_inc(s[f"{st}_xt"], 1)

            def hidden(f, k, count):
                wait(act, f"h{f}", count)
                nc.scalar.activation(hid[:, f, :], bank(k), ACT.Gelu_apprx_tanh,
                                     bias=b1_s[:, f:f + 1]).then_inc(s[f"act{f}"], 1)

            def store_y(sl):
                wait(act, "mod", sl.count(-1))
                nc.scalar.copy(yall[:, bass.ds(sl.batch(-1) * S, S)], bank(X0)).then_inc(s["ystore"], 1)

            def masked_q(a, k, h, heads):
                dst = qm[:, 0:NT * heads * P].rearrange("p (j h n) -> p j h n", j=NT, h=heads)[:, :, h, :]
                col = h if a == "a" else H0 + h
                return nc.scalar.activation(dst, bank(k).rearrange("p (j n) -> p j n", j=NT), ACT.Copy,
                                            scale=hm[:, col:col + 1])

            def load(dst, src):
                act.dma_start(dst, src).then_inc(s["w_load"], 16)

            def load_late(dst, src):
                act.dma_start(dst, src).then_inc(s["w_late"], 16)
            with nc.allow_non_contiguous_dma("weights, once"):
                load(w_o1[:], wo1.rearrange("(k p) n -> p k n", p=P))
                load(gcol_s[:], gcol)
                load_late(wr_b[:], wr.rearrange("(a n) -> a n", a=1).to_broadcast((P, P)))
                load_late(w1_s[:].rearrange("p f n -> p (f n)"), w1)
                load_late(b1_s[:], b1.rearrange("(f p) -> p f", p=P))
                load_late(w2_s[:], w2.rearrange("(f p) n -> p f n", p=P))
            act.wait_ge(s["w_pool"], 1)
            nc.scalar.activation(gve[:, 0:1], mhalf[:, 0:1], ACT.Gelu_apprx_tanh)
            act.wait_ge(s["w_pe"], 1)
            nc.scalar.copy(faT, PS[0:16, 0:P]).then_inc(s["w_act"], 1)
            act.wait_ge(s["w_late"], 16 * N_LATE)
            act.wait_ge(s["vm_zero"], 1)

            def slot_a(sl, prepare, score, complete):
                now, new, old = sl.count(0), sl.count(1), sl.count(-1)
                if prepare:
                    copy_xt("ln_f1", xt["p"], X0, new)
                if complete:
                    wait(act, "tg", old)
                    nc.scalar.copy(gt[:, 0, :], bank(X1)).then_inc(s["gt"], 1)
                if prepare:
                    copy_xt("ln_ret", xt["p"], X1, new)
                if complete:
                    copy_xt("ln_f2", xt["c"], X0, old)
                if prepare:
                    wait(act, "v_mm", new)
                    nc.scalar.copy(vv[:, :, 0:P], bank(0).rearrange("p (j n) -> p j n", j=NT)).then_inc(s["vv"], 1)
                    wait(act, "g_mm", new)
                    wait(act, "gate", now)
                    nc.scalar.activation(th[:, 0:S], bank(1), ACT.Tanh, scale=0.5).then_inc(s["tanh"], 1)
                if score:
                    wait(act, "y", now)
                    nc.scalar.activation(sq[:, 0:S], bank(4), ACT.Square).then_inc(s["sq"], 1)
                if prepare:
                    for j in range(NT):
                        blocks = vm[:, j * H0 * P:(j + 1) * H0 * P]
                        dst = bass.AP(blocks.tensor, blocks.offset, [blocks.ap[0], [P + E0, H0], [1, E0]])
                        last = nc.scalar.copy(dst, bank(0, j * P, P).rearrange("p (h e) -> p h e", h=H0))
                    last.then_inc(s["v"], 1)
                if complete:
                    copy_xt("ln_mod", xt["r"], X0, old)
                if prepare:
                    wait(act, "tqk", new)
                    nc.scalar.copy(qt[:], bank(X1)).then_inc(s["qt"], 1)
                    nc.scalar.copy(kt[:], bank(X2))
                    masked_q("a", X1, 0, H0)
                for g in range(4):
                    if complete:
                        hidden(g, (3, 0, 1, 3)[g], old)
                    if prepare:
                        last = masked_q("a", X1, 1 + g, H0)
                        if g == 3:
                            last.then_inc(s["qm"], 1)
                if complete:
                    store_y(sl)

            def slot_b(sl, prepare, score, complete):
                now, new, old = sl.count(0), sl.count(1), sl.count(-1)
                if prepare:
                    copy_xt("ln_ret", xt["p"], X0, new)
                if complete:
                    wait(act, "tg", old)
                    nc.scalar.copy(gt[:].rearrange("p k n -> p (k n)"), PS[:, X1 * BANK:(X2 + 1) * BANK]) \
                        .then_inc(s["gt"], 1)
                if prepare:
                    wait(act, "v_mm", new)
                    nc.scalar.copy(vv[:].rearrange("p j n -> p (j n)"), PS[:, 0:2 * BANK]).then_inc(s["vv"], 1)
                if score:
                    wait(act, "y", now)
                    nc.scalar.activation(sq[:], PS[:, 3 * BANK:5 * BANK], ACT.Square).then_inc(s["sq"], 1)
                if prepare:
                    for j in range(NT):
                        blocks = vm[:, j * H1 * P:(j + 1) * H1 * P]
                        dst = bass.AP(blocks.tensor, blocks.offset, [blocks.ap[0], [2 * P, 2], [P + V1, 2], [1, V1]])
                        last = nc.scalar.copy(dst, bank(j // 2, (j % 2) * VF, VF)
                                              .rearrange("p (a b e) -> p a b e", a=2, b=2))
                    last.then_inc(s["v"], 1)
                if prepare:
                    wait(act, "g_mm", new)
                    wait(act, "gate", now)
                    nc.scalar.activation(th, PS[:, X1 * BANK:(X2 + 1) * BANK], ACT.Tanh, scale=0.5) \
                        .then_inc(s["tanh"], 1)
                if complete:
                    copy_xt("ln_mod", xt["r"], X0, old)
                if prepare:
                    wait(act, "tqk", new)
                    nc.scalar.copy(kt[:], bank(2))
                    nc.scalar.copy(qt[:], bank(1))
                for g in range(4):
                    if prepare:
                        last = masked_q("b", 1, g, H1)
                        if g == 3:
                            last.then_inc(s["qm"], 1)
                    if complete:
                        hidden(g, (0, X1, X2, 0)[g], old)
                if complete:
                    store_y(sl)

            def sigmoid(total):
                act.wait_ge(s["score"], total)
                nc.scalar.activation(wcol[:], scol[:], ACT.Tanh, scale=0.5).then_inc(s["k_act"], 1)

            run_slots(act, slot_a, 0)
            sigmoid(NB)
            act.wait_ge(s["vm_zero"], 2)
            act.wait_ge(s["k_dve"], K_STEPS)
            run_slots(act, slot_b, NB)
            sigmoid(2 * NB)

            act.wait_ge(s["k_dve"], 2 * K_STEPS)
            with act.Fori(0, NB // 2) as i:
                for j in range(NT):
                    y = yall[:, bass.ds(i * 2 * S + S + j * P, P)]
                    last = nc.scalar.activation(y, y, ACT.Copy, scale=wcol[:, bass.ds(i * 2 * NT + NT + j, 1)])
                last.then_inc(s["weighted"], 1)

        @block.gpsimd
        def _(pool):
            def root(st, n, count):
                wait(pool, f"{st}_ve", count)
                nc.gpsimd.tensor_tensor(rstd[n][:], ve[n][:], mhalf[:, 0:NT], ALU.pow).then_inc(s[f"{st}_rstd"], 1)

            def group_root(n, count):
                wait(pool, "gve", count)
                nc.gpsimd.tensor_tensor(grstd[:, 0:n], gve[:, 0:n], mhalf[:, 0:n], ALU.pow) \
                    .then_inc(s["grstd"], 1)

            def sum_states(n, count):
                wait(pool, "um", count)
                nc.gpsimd.tensor_tensor(um[:, 1, 0:n], um[:, 1, 0:n], um[:, 0, 0:n], ALU.add).then_inc(s["um1"], 1)
                wait(pool, "um1", count)
                nc.gpsimd.tensor_tensor(um[:, 2, 0:n], um[:, 2, 0:n], um[:, 1, 0:n], ALU.add) \
                    .then_inc(s["state_sum"], 1)

            def tiles_of(w):
                return w[:].rearrange("p (a n) -> p a n", a=1).to_broadcast((P, NT, P))

            def router_product(st, count):
                wait(pool, f"{st}_xn", count)
                nc.gpsimd.tensor_tensor(rp[:], xn["c"][:], tiles_of(wr_b), ALU.mult).then_inc(s["rprod"], 1)

            nc.gpsimd.memset(mhalf[:], -0.5).then_inc(s["w_pool"], 1)
            nc.gpsimd.memset(ones_b[:], 1.0).then_inc(s["w_pool"], 1)
            nc.gpsimd.memset(bias_f[:], 0.0).then_inc(s["w_pool"], 1)
            nc.gpsimd.memset(bias_2[:], 0.0).then_inc(s["w_pool"], 1)
            nc.gpsimd.memset(vm[:], 0.0).then_inc(s["vm_zero"], 1)
            pool.wait_ge(s["w_step"], 1)
            nc.gpsimd.partition_all_reduce(amax[:, 1:2], amax[:, 0:1], P, bass.bass_isa.ReduceOp.max) \
                .then_inc(s["w_pool"], 1)

            def slot_a(sl, prepare, score, complete):
                now, new, old = sl.count(0), sl.count(1), sl.count(-1)
                if prepare:
                    root("ln_f1", "p", new)
                if complete:
                    wait(pool, "yn", old)
                    y4 = t2[:, 0:S].rearrange("p (j n) -> p j n", j=NT)
                    nc.gpsimd.tensor_tensor(y4, y4, tiles_of(gnw_b), ALU.mult).then_inc(s["ynw"], 1)
                    wait(pool, "ynw", old)
                    nc.gpsimd.tensor_tensor(y4, y4, tiles_of(gnb_b), ALU.add).then_inc(s["ynb"], 1)
                if score:
                    sum_states(P, now)
                if prepare:
                    root("ln_ret", "p", new)
                if complete:
                    root("ln_f2", "c", old)
                    root("ln_mod", "c", old)
                    router_product("ln_mod", old)
                if score:
                    group_root(4 * H0, now)

            def slot_b(sl, prepare, score, complete):
                now, new, old = sl.count(0), sl.count(1), sl.count(-1)
                if prepare:
                    root("ln_ret", "p", new)
                if score:
                    sum_states(VF, now)
                if complete:
                    root("ln_mod", "c", old)
                    router_product("ln_mod", old)
                if score:
                    group_root(4 * H1, now)

            pool.wait_ge(s["w_pool"], W_POOL)
            pool.wait_ge(s["w_late"], 16 * N_LATE)
            run_slots(pool, slot_a, 0)
            pool.wait_ge(s["y"], NB)
            nc.gpsimd.memset(vm[:], 0.0).then_inc(s["vm_zero"], 1)
            run_slots(pool, slot_b, NB)

            with pool.Fori(0, NB // 2) as i:
                at = bass.ds(i * 2 * S + S, S)
                pool.wait_ge(s["weighted"], pool.snap(i + 1))
                nc.gpsimd.tensor_tensor(base[:, at], base[:, at], yall[:, at], ALU.add).then_inc(s["out_pool"], 1)

        @block.vector
        def _(dve):
            def half_statistics(st, n, src):
                for j in range(NT):
                    last = nc.vector.bn_stats(st6[n][:, j, :], src[:, j, :])
                last.then_inc(s[f"{st}_stats"], 1)

            def join_halves(st, n, count):
                wait(dve, f"{st}_stats", count)
                mean_e, mean_o, m2_e, m2_o = (st6[n][:, :, k] for k in (1, 4, 2, 5))
                mean, total, diff, m2, dsq = (mv[n][:, k, :] for k in range(5))
                nc.vector.tensor_tensor(total, mean_e, mean_o, ALU.add)
                nc.vector.tensor_tensor(diff, mean_e, mean_o, ALU.subtract)
                nc.vector.scalar_tensor_tensor(m2, m2_e, P * EPS, m2_o, ALU.add, ALU.add) \
                    .then_inc(s[f"{st}_mv"], 1)
                wait(dve, f"{st}_mv", count)
                nc.vector.scalar_tensor_tensor(dsq, diff, 0.25, diff, ALU.mult, ALU.mult)
                nc.vector.tensor_scalar(mean, total, 0.5, None, ALU.mult).then_inc(s[f"{st}_sq"], 1)
                wait(dve, f"{st}_sq", count)
                nc.vector.scalar_tensor_tensor(ve[n][:], m2, 1.0 / P, dsq, ALU.mult, ALU.add) \
                    .then_inc(s[f"{st}_ve"], 1)

            def statistics(st, n, src, count):
                half_statistics(st, n, src)
                join_halves(st, n, count)

            def normalise(st, n, src, count):
                wait(dve, f"{st}_rstd", count)
                for j in range(NT):
                    last = nc.vector.tensor_scalar(xn[n][:, j, :], src[:, j, :], mv[n][:, 0, j:j + 1],
                                                   rstd[n][:, j:j + 1], ALU.subtract, ALU.mult)
                last.then_inc(s[f"{st}_xn"], 1)

            def flat(ap):
                return ap.rearrange("p j n -> p (j n)")

            def residual(k, src, dst, done, signal, count):
                wait(dve, done, count)
                nc.vector.tensor_tensor(flat(dst[:]), bank(k), flat(src[:]), ALU.add).then_inc(s[signal], 1)
                wait(dve, signal, count)

            def rotate(count):
                wait(dve, "qk", count)
                qk = PS[:, X1 * BANK:(X2 + 1) * BANK]
                swapped = qk.rearrange("p (m e) -> p m e", e=2)[:, :, ::-1]
                nc.vector.tensor_tensor(ra[:], qk, rot[:, 0], ALU.mult)
                nc.vector.tensor_tensor(rb[:].rearrange("p (m e) -> p m e", e=2), swapped,
                                        rot[:, 1].rearrange("p (m e) -> p m e", e=2), ALU.mult) \
                    .then_inc(s["prod"], 1)
                wait(dve, "prod", count)
                nc.vector.tensor_tensor(qkr[:].rearrange("p q j n -> p (q j n)"), ra[:], rb[:], ALU.add) \
                    .then_inc(s["qkr"], 1)

            def causal(c, k, heads, sl):
                wait(dve, f"sc{c}", sl.count(0))
                if c < 2:
                    wait(dve, "y", sl.count(-1))
                else:
                    wait(dve, f"av{c - 2}", sl.count(0))
                m = tri[:].rearrange("p (a n) -> p a n", a=1).to_broadcast((P, heads, P))
                nc.vector.tensor_tensor(sc[c % 2][:, 0:heads * P].rearrange("p (h n) -> p h n", h=heads),
                                        PS[:, k * BANK:k * BANK + heads * P].rearrange("p (h n) -> p h n", h=heads),
                                        m, ALU.mult).then_inc(s[f"msk{c}"], 1)

            def mask_states(k, width, bd, count):
                wait(dve, "state", count)
                nc.vector.tensor_tensor(um[:, :, 0:width],
                                        PS[:, k * BANK:k * BANK + 3 * width].rearrange("p (c n) -> p c n", c=3),
                                        bd[:].rearrange("p (a n) -> p a n", a=1).to_broadcast((P, 3, width)),
                                        ALU.mult).then_inc(s["um"], 1)

            def keep_base(sl):
                nc.vector.scalar_tensor_tensor(base[:, bass.ds(sl.batch(-1) * S, S)], flat(xn["c"][:]), 0.5,
                                               flat(x2[:]), ALU.mult, ALU.add).then_inc(s["base"], 1)

            def router_sum(sl):
                wait(dve, "rprod", sl.count(-1))
                nc.vector.tensor_reduce(scol[:, bass.ds(sl.batch(-1) * NT, NT)], rp[:], AX.X, ALU.add) \
                    .then_inc(s["score"], 1)

            def head_sums(heads, width, count):
                n = NT * heads
                wait(dve, "sq", count)
                nc.vector.tensor_reduce(gve[:, 0:n], sq[:, 0:n * width].rearrange("p (h e) -> p h e", e=width),
                                        AX.X, ALU.add).then_inc(s["var"], 1)
                wait(dve, "var", count)
                nc.vector.tensor_scalar(gve[:, 0:n], gve[:, 0:n], 1.0 / width, EPS, ALU.mult, ALU.add) \
                    .then_inc(s["gve"], 1)

            def head_norm(k, heads, width, count):
                n = NT * heads
                wait(dve, "grstd", count)
                nc.vector.tensor_tensor(t2[:, 0:n * width].rearrange("p (h e) -> p h e", e=width),
                                        PS[:, k * BANK:k * BANK + n * width].rearrange("p (h e) -> p h e", e=width),
                                        grstd[:, 0:n].rearrange("p (h a) -> p h a", a=1).to_broadcast((P, n, width)),
                                        ALU.mult).then_inc(s["yn"], 1)

            def kept_tiles(sl, d):
                return base[:, bass.ds(sl.batch(d) * S, S)].rearrange("p (j n) -> p j n", j=NT)

            def combine(sl, d, dst, signal):
                for j in range(NT):
                    at = sl.batch(d) * S + j * P
                    last = nc.vector.scalar_tensor_tensor(
                        dst[:, j, :], yall[:, bass.ds(at, P)], wcol[:, bass.ds(sl.batch(d) * NT + j, 1)],
                        base[:, bass.ds(at, P)], ALU.mult, ALU.add)
                last.then_inc(s[signal], 1)

            def ahead(sl):
                return not isinstance(sl.k, int) or sl.k + 2 < NB

            def input_statistics(p, landed, count):
                wait(dve, f"x_in{p}", landed)
                statistics("ln_f1", "p", xin[p], count)

            input_statistics(0, 16, 1)

            steps = [0]

            def step(ins):
                steps[0] += 1
                ins.then_inc(s["w_step"], 1)
                dve.wait_ge(s["w_step"], steps[0])

            dve.wait_ge(s["w_load"], 16 * N_LOADS)
            step(nc.vector.tensor_reduce(amax[:, 0:1], kern_s, AX.X, ALU.max, apply_absolute_value=True))
            dve.wait_ge(s["w_pool"], 4)
            step(nc.vector.tensor_scalar(brow[0:1, 0, :], brow[0:1, 0, :], 0.5, None, ALU.mult))
            for n, dst in enumerate((bias_f, bias_2)):
                src = brow[0:1, n, :]
                for part in range(3):
                    row = dst[32 * part:32 * part + 1, 0, :]
                    step(nc.vector.tensor_copy(row, src))
                    if part < 2:
                        step(nc.vector.tensor_tensor(bres[0:1, n, part, :], src, row, ALU.subtract))
                        src = bres[0:1, n, part, :]
                    step(nc.vector.tensor_copy(dst[32 * part:32 * part + 1, 1:NT, :],
                                               dst[32 * part:32 * part + 1, 0:1, :].to_broadcast((1, NT - 1, P))))
            wv = w_qkvg[:, 2, :].rearrange("p (h e) -> p h e", h=H0)
            step(nc.vector.tensor_reduce(vmean[:], wv, AX.X, ALU.add))
            step(nc.vector.tensor_scalar(vmean[:], vmean[:], -1.0 / E0, None, ALU.mult))
            step(nc.vector.tensor_tensor(wv, wv, vmean[:].rearrange("p (h a) -> p h a", a=1)
                                         .to_broadcast((P, H0, E0)), ALU.add))
            step(nc.vector.tensor_scalar(w_o0[:], w_o0[:], 0.5, None, ALU.mult))
            step(nc.vector.tensor_scalar(w_o1[:], w_o1[:], gcol_s[:, 0:1], 0.5, ALU.mult, ALU.mult))
            step(nc.vector.tensor_copy(blkb[:], blk))
            dve.wait_ge(s["w_pool"], 5)
            step(nc.vector.tensor_scalar(amax[:, 2:3], amax[:, 1:2], 1.0 / 7.0, None, ALU.mult))
            step(nc.vector.reciprocal(amax[:, 3:4], amax[:, 2:3]))
            big_round = 1.5 * 2.0 ** 23
            step(nc.vector.tensor_scalar(w_ffn[:], kern_s, amax[:, 3:4], big_round, ALU.mult, ALU.add))
            step(nc.vector.tensor_scalar(w_ffn[:], w_ffn[:], -big_round, 7.0, ALU.add, ALU.min))
            step(nc.vector.tensor_scalar(w_ffn[:], w_ffn[:], -8.0, amax[:, 2:3], ALU.max, ALU.mult))
            dve.wait_ge(s["w_pe"], 2)
            step(nc.vector.tensor_tensor(w_ffn[:], w_ffn[:], bank(1, 0, P), ALU.add))
            step(nc.vector.tensor_scalar(w_ffn[:], w_ffn[:], 0.5, None, ALU.mult))
            assert steps[0] == W_STEPS, steps[0]

            def slot_a(sl, prepare, score, complete):
                now, new, old = sl.count(0), sl.count(1), sl.count(-1)
                xi, x_new, x_old = xin[sl.buf(1)], x1[sl.buf(1)], x1[sl.buf(-1)]
                if complete:
                    head_norm(4, H0, E0, old)
                if prepare:
                    normalise("ln_f1", "p", xi, new)
                if score:
                    causal(0, 0, H0, sl)
                if complete:
                    wait(dve, "ynb", old)
                    nc.vector.tensor_tensor(t2[:, 0:S], t2[:, 0:S], gate[sl.buf(-1)][:, 0:S], ALU.mult) \
                        .then_inc(s["gy"], 1)
                if score:
                    causal(1, 2, H0, sl)
                if complete:
                    residual(X0, x_old, x2, "wo", "x2", old)
                if prepare:
                    residual(X2, xi, x_new, "ffn1", "x1", new)
                    statistics("ln_ret", "p", x_new, new)
                if complete:
                    half_statistics("ln_f2", "c", x2)
                if prepare:
                    normalise("ln_ret", "p", x_new, new)
                if complete:
                    join_halves("ln_f2", "c", old)
                if score:
                    causal(2, 0, H0, sl)
                if complete:
                    normalise("ln_f2", "c", x2, old)
                if score:
                    causal(3, 2, H0, sl)
                if complete:
                    residual(X0, x2, x2, "ffn2", "x3", old)
                    statistics("ln_mod", "c", x2, old)
                if prepare:
                    rotate(new)
                if complete:
                    normalise("ln_mod", "c", x2, old)
                if prepare:
                    wait(dve, "tanh", new)
                    nc.vector.scalar_tensor_tensor(gate[sl.buf(1)][:, 0:S], th[:, 0:S], 1.0, bank(1),
                                                   ALU.add, ALU.mult).then_inc(s["gate"], 1)
                if score:
                    head_sums(H0, E0, now)
                if prepare:
                    mask_states(2, P, bd0, new)
                if complete:
                    wait(dve, "ln_mod_xn", old)
                    keep_base(sl)
                if ahead(sl):
                    input_statistics(sl.buf(2), sl.loads, sl.count(2))
                if complete:
                    router_sum(sl)
                if prepare:
                    wait(dve, "qt", new)
                    blocks = qm[:].rearrange("p (j h n) -> p j h n", j=NT, h=H0)
                    for h in range(ACT_HEADS, H0):
                        last = nc.vector.tensor_scalar(blocks[:, :, h, :], qt[:].rearrange("p (j n) -> p j n", j=NT),
                                                       hm[:, h:h + 1], None, ALU.mult)
                    last.then_inc(s["qm_dve"], 1)

            def slot_b(sl, prepare, score, complete):
                now, new, old = sl.count(0), sl.count(1), sl.count(-1)
                if prepare:
                    normalise("ln_ret", "p", kept_tiles(sl, 1), new)
                if score:
                    causal(0, 0, H1, sl)
                    causal(1, 1, H1, sl)
                if score:
                    causal(2, 2, H1, sl)
                if complete:
                    residual(X0, kept_tiles(sl, -1), x2, "wo", "x2", old)
                    statistics("ln_mod", "c", x2, old)
                if score:
                    causal(3, 2, H1, sl)
                if prepare:
                    rotate(new)
                if complete:
                    normalise("ln_mod", "c", x2, old)
                if prepare:
                    wait(dve, "tanh", new)
                    nc.vector.scalar_tensor_tensor(gate[sl.buf(1)][:], th, 1.0, PS[:, X1 * BANK:(X2 + 1) * BANK],
                                                   ALU.add, ALU.mult).then_inc(s["gate"], 1)
                if score:
                    head_sums(H1, V1, now)
                if complete:
                    wait(dve, "ln_mod_xn", old)
                    keep_base(sl)
                if ahead(sl):
                    combine(sl, 2, kept_tiles(sl, 2), "x1")
                    wait(dve, "x1", sl.count(2))
                if complete:
                    router_sum(sl)
                if ahead(sl):
                    statistics("ln_ret", "p", kept_tiles(sl, 2), sl.count(2))
                if score:
                    head_norm(3, H1, V1, now)
                    wait(dve, "yn", now)
                    nc.vector.tensor_tensor(t2[:], t2[:], gate[sl.buf(0)][:], ALU.mult).then_inc(s["gy"], 1)
                if prepare:
                    mask_states(X1, VF, bd1, new)

            def topk(n0, total, pes, act_done):
                n = [n0]

                def step(ins):
                    n[0] += 1
                    ins.then_inc(s["k_dve"], 1)
                    dve.wait_ge(s["k_dve"], n[0])

                dve.wait_ge(s["score"], total)
                step(nc.vector.tensor_copy(srep, scol[:].rearrange("p (b j a) -> p j b a", j=NT, a=1)
                                           .to_broadcast((P, NT, NB, REP))))
                step(nc.vector.memset(zero, 0.0))
                dve.wait_ge(s["k_pe"], pes + 1)
                step(nc.vector.tensor_reduce(amax[:, 0:1], bank(2), AX.X, ALU.max, apply_absolute_value=True))
                step(nc.vector.tensor_scalar(amax[:, 0:1], amax[:, 0:1], 1e-30, None, ALU.max))
                step(nc.vector.tensor_scalar(amax[:, 1:2].bitcast(I32), amax[:, 0:1].bitcast(I32), 0x7f800000, None,
                                             ALU.bitwise_and))
                step(nc.vector.tensor_scalar(amax[:, 1:2], amax[:, 1:2], 2.0, None, ALU.mult))
                step(nc.vector.reciprocal(amax[:, 2:3], amax[:, 1:2]))
                step(nc.vector.tensor_scalar(srow, bank(2), amax[:, 2:3], None, ALU.mult))
                lo, hi, thr, cnt = amax[:, 0:1], amax[:, 1:2], amax[:, 2:3], amax[:, 3:4]
                step(nc.vector.memset(lo, -1.0))
                assert n[0] - n0 == K_HEAD
                for r in range(ROUNDS):
                    width = 2.0 / REP ** (r + 1)
                    step(nc.vector.tensor_tensor(thr, rs[:, r:r + 1], lo, ALU.add))
                    step(nc.vector.tensor_scalar(msk_a, srow, thr, None, ALU.is_ge, ALU.add, accum_out=cnt))
                    step(nc.vector.tensor_scalar(rankb.bitcast(BF16)[:, 0:1], cnt, float(TOPK), None, ALU.is_ge))
                    dve.wait_ge(s["k_pe"], pes + r + 2)
                    if r == ROUNDS - 1:
                        step(nc.vector.tensor_scalar(hi, bank(4, 0, 1), 1.0, width, ALU.add, ALU.mult))
                        step(nc.vector.tensor_tensor(hi, hi, lo, ALU.add))
                    step(nc.vector.scalar_tensor_tensor(lo, bank(4, 0, 1), width, lo, ALU.mult, ALU.add))
                step(nc.vector.tensor_scalar(msk_a, srow, hi, None, ALU.is_ge, ALU.add, accum_out=cnt))
                step(nc.vector.scalar_tensor_tensor(msk_b, srow, lo, msk_a, ALU.is_ge, ALU.subtract))
                step(nc.vector.tensor_scalar(cnt, cnt, -1.0, float(TOPK), ALU.mult, ALU.add))
                step(nc.vector.tensor_tensor_scan(pre, msk_b, zero, 0.0, ALU.add, ALU.add))
                step(nc.vector.scalar_tensor_tensor(pre, pre, cnt, msk_b, ALU.is_le, ALU.mult))
                step(nc.vector.tensor_tensor(msk_a, msk_a, pre, ALU.add))
                dve.wait_ge(s["k_act"], act_done)
                step(nc.vector.tensor_scalar(wcol[:], wcol[:], 1.0, 0.25, ALU.add, ALU.mult))
                dve.wait_ge(s["k_pe"], pes + ROUNDS + 2)
                w3 = wcol[:].rearrange("p (b j) -> p j b", j=NT)
                m3 = bank(2).rearrange("p (j b r) -> p j b r", j=NT, b=NB)[:, :, :, 0]
                step(nc.vector.tensor_tensor(w3, m3, w3, ALU.mult))
                dve.wait_ge(s["ystore"], total)
                assert n[0] - n0 == K_STEPS, n[0] - n0

            dve.wait_ge(s["w_late"], 16 * N_LATE)
            run_slots(dve, slot_a, 0, loads=True)
            dve.wait_ge(s["base"], NB)
            topk(0, NB, 0, 1)
            dve.wait_ge(s["rot_in"], 16)
            first = Slot(0, [], 0)
            combine(first, 0, kept_tiles(first, 0), "x1")
            dve.wait_ge(s["x1"], NB + 1)
            statistics("ln_ret", "p", kept_tiles(first, 0), NB + 1)
            run_slots(dve, slot_b, NB)
            dve.wait_ge(s["base"], 2 * NB)
            topk(K_STEPS, 2 * NB, ROUNDS + 2, 2)

            with dve.Fori(0, NB // 2) as i:
                even = Slot(i * 2, [], 0)
                combine(even, 0, kept_tiles(even, 0), "out_dve")


W_STEPS = 8 + 1 + 2 * (3 + 2 + 3) + 3 + 3
W_POOL = 5
K_HEAD, K_ROUND = 9, 4
K_STEPS = K_HEAD + ROUNDS * K_ROUND + 2 + 8


def tables():
    f = np.float32
    pos = np.arange(S, dtype=f)

    def lay(t):
        return t.reshape(NT, P, -1).transpose(1, 0, 2)

    def signed(sin):
        out = np.repeat(sin, 2, axis=-1)
        out[..., 0::2] *= -1
        return out

    half = E0 // 2
    vec = ((np.arange(0, E0, 2, dtype=f) + f(0.4 * E0)) / f(1.4 * E0)).astype(np.float64)
    inv = f(1) / (f(10000) ** (np.arange(half, dtype=f) / f(half)))
    ang = (pos[:, None] * inv[None, :]).astype(np.float64)
    gam = (f(1) - np.exp(np.linspace(np.log(1 / 32), np.log(1 / 64), H0).astype(f))).astype(np.float64)
    mid = pos.astype(np.float64) - S / 2
    r0 = np.zeros((2, S, 2, H0, E0))
    for q, sign in ((0, 1.0), (1, -1.0)):
        size = vec[None, None, :] ** (sign * mid[:, None, None] / 64) * gam[None, :, None] ** (sign * mid[:, None, None])
        r0[0, :, q] = np.repeat(np.cos(ang)[:, None, :] * size, 2, axis=-1)
        r0[1, :, q] = signed(np.sin(ang)[:, None, :] * size)
    inv = f(1) / (f(10000) ** (np.arange(0, K1, 2, dtype=f) / f(K1)))
    ang = (pos[:, None] * inv[None, :]).astype(np.float64)
    gam = 1.0 - 2.0 ** (-5.0 - np.arange(H1))
    r1 = np.zeros((2, S, 2, H1, K1))
    for q, sign in ((0, 1.0), (1, -1.0)):
        size = gam[None, :, None] ** (sign * mid[:, None, None]) * (K1 ** -0.5 if q == 0 else 1.0)
        r1[0, :, q] = np.repeat(np.cos(ang)[:, None, :] * size, 2, axis=-1)
        r1[1, :, q] = signed(np.sin(ang)[:, None, :] * size)

    def rot(r):
        return np.stack([lay(r[a, :, q].reshape(S, P)) for a in range(2) for q in range(2)], axis=1).reshape(P, -1).astype(f)

    i = np.arange(P)
    return {
        "ident": np.eye(P, dtype=f),
        "tri": (i[:, None] <= i[None, :]).astype(f),
        "bd0": (i[:, None] // E0 == i[None, :] // E0).astype(f),
        "bd1": (i[:, None] // K1 == np.arange(VF)[None, :] // V1).astype(f),
        "hm": np.concatenate([i[:, None] // E0 == np.arange(H0), i[:, None] // K1 == np.arange(H1)], axis=1).astype(f),
        "rot0": rot(r0), "rot1": rot(r1),
        "blk": (i[:, None] // REP == i[None, :] // REP).astype(f),
        "rs": ((i % REP + 1)[:, None] * 2.0 / REP ** np.arange(1, ROUNDS + 1)[None, :]).astype(f),
    }


def kernel(**inputs):
    import concourse.bacc as _bacc
    from concourse.bass_utils import run_bass_kernel_spmd as _run

    a = {k: np.ascontiguousarray(v) for k, v in inputs.items()}

    def paired(w):
        return np.ascontiguousarray(w.reshape(H1, 2, K1 // 2, P).transpose(3, 0, 2, 1).reshape(P, P))

    arrays = {
        "x": a["L0_attn_X"], "wq0": a["L0_attn_W_Q"], "wk0": a["L0_attn_W_K"], "wv0": a["L0_attn_W_V"],
        "wg0": a["L0_attn_W_G"], "wo0": a["L0_attn_W_O"], "gnw": a["L0_attn_gn_weight"], "gnb": a["L0_attn_gn_bias"],
        "kern": a["L0_ffn_kernel"], "bias": a["L0_ffn_bias"], "fa": a["L0_ffn_a"], "fb": a["L0_ffn_b"],
        "wq1": paired(a["L1_attn_Wq"]), "wk1": paired(a["L1_attn_Wk"]),
        "wv1": np.ascontiguousarray(a["L1_attn_Wv"].T), "wg1": np.ascontiguousarray(a["L1_attn_Wg"].T),
        "wo1": np.ascontiguousarray(a["L1_attn_Wo"].T),
        "gcol": np.ascontiguousarray(np.tile(a["L1_attn_gnorm_w"], P // V1).reshape(P, 1)),
        "wr": a["L1_ffn_w_router"], "w1": a["L1_ffn_W1"], "b1": a["L1_ffn_b1"], "w2": a["L1_ffn_W2"],
        "b2": a["L1_ffn_b2"], **tables(),
    }
    nc = _bacc.Bacc("TRN2", target_bir_lowering=False, num_devices=1)
    maps, args = {}, []
    for name, v in arrays.items():
        maps[f"in_{name}"] = v
        args.append(nc.dram_tensor(f"in_{name}", v.shape, mybir.dt.from_np(v.dtype), kind="ExternalInput").ap())
    args.append(nc.dram_tensor("out_x", a["L0_attn_X"].shape, F32, kind="ExternalOutput").ap())
    program(nc, *args)
    r = _run(nc, [maps], core_ids=[0])
    return r.results[0]["out_x"]
```
